# Optimizing a Trainium2 kernel written in Bass

```python
import numpy as np
import jax
import jax.numpy as jnp

def _softmax(x, axis=-1):
    return jax.nn.softmax(x, axis=axis)
def _gelu(x):
    return jax.nn.gelu(x, approximate=True)
def _silu(x):
    return jax.nn.silu(x)
def _sigmoid(x):
    return jax.nn.sigmoid(x)
def _layernorm(x, axis=-1, eps=1e-5):
    m = jnp.mean(x, axis=axis, keepdims=True)
    v = jnp.var(x, axis=axis, keepdims=True)
    return (x - m) / jnp.sqrt(v + eps)
def _scatter_add(tgt, idx, src, axis=0):
    return tgt.at[idx].add(src)
def _segment_sum(src, seg, n):
    return jax.ops.segment_sum(src, seg, n)

kernel_name = 'mk_adj_resnorm_d1_adj_256_08f4f2'

def setup_inputs(seed: int = 0):
    np.random.seed(seed)
    _w = jnp.asarray
    def _rec_inputs():
        import jax
        import jax.numpy as jnp
        _gk = jax.random.key(seed)
        x = -0.0005207 + 1.001 * jax.random.normal(jax.random.fold_in(_gk, 1), (8, 2048, 256), jnp.float32)
        _a = jax.random.bernoulli(jax.random.fold_in(_gk, 2), 0.015625, (8, 2048, 2048))
        adj = _a.astype(jnp.int32)
        return x, adj
    x, adj = _rec_inputs()
    def _L0_gnn_setup():
        import jax, jax.numpy as jnp
        import numpy as np
        B, N, D = (8, 1024, 256)
        H, HO = (4, 64)
        T = 5
        NEG = -1000000000.0
        EPS = 1e-06
        key = jax.random.key(seed)
        ks = jax.random.split(key, 6)
        nodes_embed = jax.random.normal(ks[0], (B, N, D), dtype=jnp.float32)
        node_adj = jax.random.randint(ks[1], (B, N, N), 0, T + 1)
        W = jax.random.normal(ks[2], (H, D, HO), dtype=jnp.float32) * (1.0 / np.sqrt(D))
        a_src = jax.random.normal(ks[3], (H, T, HO), dtype=jnp.float32) * 0.1
        a_dst = jax.random.normal(ks[4], (H, T, HO), dtype=jnp.float32) * 0.1
        bias = jnp.zeros((H, HO), dtype=jnp.float32)
        ln_gamma = jnp.ones((H, HO), dtype=jnp.float32)
        ln_beta = jnp.zeros((H, HO), dtype=jnp.float32)
        return {'nodes_embed': nodes_embed, 'node_adj': node_adj, 'W': W, 'a_src': a_src, 'a_dst': a_dst, 'bias': bias, 'ln_gamma': ln_gamma, 'ln_beta': ln_beta}
    _L0_gnn_all = _L0_gnn_setup()
    _L0_gnn_in = {k: v for k, v in _L0_gnn_all.items() if k in ('W', 'a_src', 'a_dst', 'bias', 'ln_gamma', 'ln_beta', )}
    del _L0_gnn_all

    return {
        "x": x,
        "adj": adj,
        "L0_gnn_W": _L0_gnn_in["W"],
        "L0_gnn_a_src": _L0_gnn_in["a_src"],
        "L0_gnn_a_dst": _L0_gnn_in["a_dst"],
        "L0_gnn_bias": _L0_gnn_in["bias"],
        "L0_gnn_ln_gamma": _L0_gnn_in["ln_gamma"],
        "L0_gnn_ln_beta": _L0_gnn_in["ln_beta"],
    }

def reference(x, adj, L0_gnn_W, L0_gnn_a_src, L0_gnn_a_dst, L0_gnn_bias, L0_gnn_ln_gamma, L0_gnn_ln_beta):
    import jax
    import jax.numpy as jnp
    def _L0_gnn_ref(nodes_embed, node_adj, W, a_src, a_dst, bias, ln_gamma, ln_beta):
        import jax, jax.numpy as jnp
        import numpy as np
        B, N, D = (8, 1024, 256)
        H, HO = (4, 64)
        T = 5
        NEG = -1000000000.0
        EPS = 1e-06
        h = jnp.einsum('bnd,hde->bhne', nodes_embed, W)
        e_src = jnp.einsum('bhne,hte->bhtn', h, a_src)
        e_dst = jnp.einsum('bhne,hte->bhtn', h, a_dst)
        n_types = a_src.shape[1]
        weight = jnp.zeros(h.shape[:2] + (h.shape[2], h.shape[2]), dtype=h.dtype)
        for t in range(n_types):
            mask = (node_adj == t + 1).astype(h.dtype)[:, None]
            weight = weight + mask * (e_src[:, :, t, :, None] + e_dst[:, :, t, None, :])
        weight = jax.nn.leaky_relu(weight, negative_slope=0.01)
        weight = jnp.where(node_adj[:, None] == 0, NEG, weight)
        attention = jax.nn.softmax(weight, axis=-1)
        dst = jnp.einsum('bhij,bhje->bhie', attention, h) + bias[None, :, None, :]
        out = jax.nn.relu(dst) + h
        mu = out.mean(axis=-1, keepdims=True)
        var = out.var(axis=-1, keepdims=True)
        out = (out - mu) / jnp.sqrt(var + EPS) * ln_gamma[None, :, None, :] + ln_beta[None, :, None, :]
        b, hh, n, e = out.shape
        return out.transpose(0, 2, 1, 3).reshape(b, n, hh * e)

    x = _layernorm(x + _L0_gnn_ref(x, adj, L0_gnn_W, L0_gnn_a_src, L0_gnn_a_dst, L0_gnn_bias, L0_gnn_ln_gamma, L0_gnn_ln_beta), axis=-1)
    return x


_drawn_inputs = setup_inputs


def setup_inputs(seed=0):
    import zlib

    import numpy as np

    out = dict(_drawn_inputs(seed))
    spreads = {'L0_gnn_bias': (0.0, 0.1), 'L0_gnn_ln_gamma': (1.0, 0.2), 'L0_gnn_ln_beta': (0.0, 0.1)}
    factors = {}
    for name, (base, spread) in spreads.items():
        noise = np.random.default_rng([zlib.crc32(name.encode()), seed]).standard_normal(out[name].shape)
        drawn = base * np.exp(spread * noise) if base else spread * noise
        out[name] = jnp.asarray(drawn.astype(out[name].dtype))
    for name, factor in factors.items():
        out[name] = (out[name] * factor).astype(out[name].dtype)
    return out
```

```python
from contextlib import ExitStack

import concourse.bass as bass
from concourse import mybir

P = 128
F16 = mybir.dt.float16
F32 = mybir.dt.float32
I32 = mybir.dt.int32
ALU = mybir.AluOpType
ACT = mybir.ActivationFunctionType
AX = mybir.AxisListType
RMAX = bass.bass_isa.ReduceOp.max

LEAK = 0.01
EPS_HEAD = 1e-6
EPS_ROW = 1e-5

V_SCALE = 4.0
LN_V_SCALE = 1.3862943611198906
EXP_SQ = 42.0
H_SQ = 600.0
DEN_LEAST = 1e-6

TPB = 4
A16_SLOTS = 4
NA_SLOTS = 8


def dims(x, adj, W):
    B, N, D = x.shape
    H, E = W.shape[0], W.shape[2]
    return B, N, D, H, E


def main_path(nc, io, viol_i, sems):
    x, adj, W = io["x"], io["adj"], io["W"]
    B, N, D, H, E = dims(x, adj, W)
    JT = N // P
    NT = B * JT
    BLK = TPB * P
    NB = NT // TPB
    KD = D // P
    E1 = E + 1
    HC = D + 4 * H
    CH = N // 2
    CPB = 2 * TPB
    BPB = JT // TPB
    HALF = JT // 2
    HP_NA = D + 2 * H
    RW = 3 * E1
    assert H == TPB == 4 and D == 2 * P and JT == 16 and E == 64

    x_t = x.rearrange("b (t p) d -> p (b t) d", p=P)
    out_t = io["out"].rearrange("b (t p) d -> p (b t) d", p=P)
    adj_t = adj.rearrange("b (t p) n -> p (b t) n", p=P)
    hu_t = io["hu"].rearrange("(t p) c -> p t c", p=P)

    with ExitStack() as ctx:
        def sb(name, shape, dt=F32):
            return ctx.enter_context(nc.sbuf_tensor(name, shape, dt))

        def psum(name, shape, dt=F32):
            return ctx.enter_context(nc.psum_tensor(name, shape, dt))

        def sem(name):
            return sems.enter_context(nc.semaphore(name))

        ident = sb("ident", [P, P])
        sel = sb("sel", [TPB * H, TPB * H, P], F16)
        wa = sb("wa", [P, KD, D + 2 * H])
        bias_bc = sb("bias_bc", [P, D])
        gamma_bc = sb("gamma_bc", [P, D])
        beta_bc = sb("beta_bc", [P, D])
        neg_half = sb("neg_half", [P, 1])
        ln_scale = sb("ln_scale", [P, 1])
        exponent = sb("exponent", [P, TPB * H])
        xin = sb("xin", [P, 2, D])
        xT = sb("xT", [P, KD, P])
        hb = sb("hb", [P, H, E1])
        vh32 = sb("vh32", [P, 2, H, E1])
        vh = sb("vh", [P, 2 * JT, H, 2, 2, E1], F16)
        bcol = sb("bcol", [P, 2 * JT, H])
        na_c = sb("na_c", [P, H, TPB])
        na_t = sb("na_t", [TPB * H, NA_SLOTS, 2, P], F16)
        hu_out = sb("hu_out", [P, TPB, HC])
        hu_in = sb("hu_in", [P, 2, TPB, HC])
        a16 = sb("a16", [P, A16_SLOTS, CH], F16)
        mt = sb("mt", [P, 2, JT, BLK], F16)
        g_sb = sb("g_sb", [P, 2, JT, BLK], F16)
        dens = sb("dens", [P, 2, 2, 3])
        den_e = sb("den_e", [P, 2, 2])
        den_m = sb("den_m", [P, 2, 2, 2])
        rden_in = sb("rden_in", [P, TPB])
        rden = sb("rden", [P, TPB])
        cw = sb("cw", [P, 2, TPB])
        m_sum = sb("m_sum", [P, 2, 2, E])
        t1 = sb("t1", [P, TPB, E])
        e2 = sb("e2", [P, TPB, E])
        att = sb("att", [P, 2, TPB, D])
        x_res = sb("x_res", [P, 2, TPB, D])
        sq = sb("sq", [P, TPB, D])
        fin = sb("fin", [P, TPB, D])
        s_head = sb("s_head", [P, 2, TPB * H])
        m_head = sb("m_head", [P, TPB * H])
        r_head = sb("r_head", [P, TPB * H])
        s_row = sb("s_row", [P, 2, TPB])
        m_row = sb("m_row", [P, TPB])
        r_row = sb("r_row", [P, TPB])
        n_row = sb("n_row", [P, TPB])
        scrap = sb("scrap", [P, 2, CH], F16)
        scrap_e = sb("scrap_e", [P, 2 * H])
        scrap_h = sb("scrap_h", [P, H * E1], F16)
        met_adj = sb("met_adj", [P, NB * CPB])
        met_exp = sb("met_exp", [P, NT])
        met_h = sb("met_h", [P, NT])
        met_den = sb("met_den", [P, NB * TPB * H])
        worst = sb("worst", [P, 4])
        broken = sb("broken", [P, 5])
        broken_all = sb("broken_all", [P, 1])

        acc = psum("acc", [P, 4, 512])
        na = psum("na", [P, 2, 512])
        turn = psum("turn", [P, 512])
        hp = psum("hp", [P, 512])

        consts_in = sem("consts_in")
        consts_set = sem("consts_set")
        wa_done = sem("wa_done")
        x_in = [sem(f"x_in{i}") for i in range(2)]
        x_turned = sem("x_turned")
        xT_copied = sem("xT_copied")
        h_made = sem("h_made")
        exps_made = sem("exps_made")
        h_read_act = sem("h_read_act")
        h_read_dve = sem("h_read_dve")
        na_turned = sem("na_turned")
        na_hi_done = sem("na_hi_done")
        na_split = sem("na_split")
        na_made = sem("na_made")
        hu_stored = sem("hu_stored")
        hb_made = sem("hb_made")
        vh32_made = sem("vh32_made")
        vh_hi_done = sem("vh_hi_done")
        vh_done = sem("vh_done")
        a16_in = [sem(f"a16_in{i}") for i in range(A16_SLOTS)]
        adj_checked = sem("adj_checked")
        turned = [sem(f"turned{i}") for i in range(A16_SLOTS)]
        g_made = sem("g_made")
        unit_done = sem("unit_done")
        dens_read = sem("dens_read")
        m_read = sem("m_read")
        den_step = sem("den_step")
        den_made = sem("den_made")
        rden_safe = sem("rden_safe")
        rden_made = sem("rden_made")
        cw_made = sem("cw_made")
        t1_made = sem("t1_made")
        e2_made = sem("e2_made")
        att_made = sem("att_made")
        res_in = sem("res_in")
        o_made = sem("o_made")
        s1_made = sem("s1_made")
        mean_made = sem("mean_made")
        cent_made = sem("cent_made")
        sq_made = sem("sq_made")
        s2_made = sem("s2_made")
        norm_step = sem("norm_step")
        z_made = sem("z_made")
        s3_made = sem("s3_made")
        m2_made = sem("m2_made")
        s4_made = sem("s4_made")
        r2_made = sem("r2_made")
        fin_made = sem("fin_made")
        out_stored = sem("out_stored")
        met_done = sem("met_done")
        viol_step = sem("viol_step")
        viol_step_dve = sem("viol_step_dve")
        stood = {e.engine: sem(f"stood_{n}") for n, e in
                 (("sp", nc.sync), ("pool", nc.gpsimd), ("act", nc.scalar), ("dve", nc.vector), ("pe", nc.tensor))}

        block = ctx.enter_context(nc.Block())

        def region(u_slot, it):
            c = (it % 2) * RW
            return acc[:, 2 * u_slot + it // 2, c:c + RW]

        def regions(u_slot, c0, c1):
            r = acc[:, 2 * u_slot:2 * u_slot + 2, 0:2 * RW]
            return r.rearrange("p k (i c) -> p k i c", c=RW)[:, :, :, c0:c1]

        def batch_slot(t):
            return t % (2 * JT)

        def tail_of(ap, n):
            k = len(ap.shape)
            return ap.unsqueeze(k).to_broadcast([*ap.shape, n])

        def stand(eng):
            eng.sem_inc(stood[eng.engine], 1)

        na_turn = hp[0:TPB * H, HP_NA:HP_NA + P]


        @block.sync
        def _(sp):
            def load_x(t, slot, turned_before):
                sp.wait_ge(x_turned, turned_before)
                stand(sp)
                sp.dma_start(xin[:, slot, :].unsqueeze(1), x_t[:, bass.ds(t, 1), :]).then_inc(x_in[slot], 16)

            def transpose_chunk(g, k, mt_slot):
                slot = k % A16_SLOTS
                it, half = k // 2, k % 2
                sp.wait_ge(a16_in[slot], (g * (CPB // A16_SLOTS) + k // A16_SLOTS + 1) * 16)
                stand(sp)
                dst = mt[:, mt_slot, half * HALF:(half + 1) * HALF, it * P:(it + 1) * P]
                sp.dma_start_transpose(dst, a16[:, slot, :]).then_inc(turned[slot], 16)

            def load_residual(g):
                sp.wait_ge(res_in, g * 32)
                sp.wait_ge(hu_stored, g * 16 + 16)
                stand(sp)
                dst = hu_in[:, bass.ds(g % 2, 1), :, :].rearrange("p a t c -> p (a t) c")
                sp.dma_start(dst, hu_t[:, bass.ds(g * TPB, TPB), :]).then_inc(res_in, 16)
                dst = x_res[:, bass.ds(g % 2, 1), :, :].rearrange("p a t c -> p (a t) c")
                sp.dma_start(dst, x_t[:, bass.ds(g * TPB, TPB), :]).then_inc(res_in, 16)

            def store_hu(p):
                sp.wait_ge(h_read_act, p * TPB + TPB)
                stand(sp)
                sp.dma_start(hu_t[:, bass.ds(p * TPB, TPB), :], hu_out[:, :, :]).then_inc(hu_stored, 16)

            sp.dma_start(ident[:], io["eye"]).then_inc(consts_in, 16)
            for k in range(KD):
                dst = wa[:, k, 0:D].rearrange("p (h e) -> p h e", h=H)
                src = W.rearrange("h (k p) e -> k p h e", p=P)[k]
                sp.dma_start(dst, src).then_inc(consts_in, 16)
            for tile, src in ((bias_bc, io["bias"]), (gamma_bc, io["gamma"]), (beta_bc, io["beta"])):
                dst = tile[:].rearrange("p (h e) -> p h e", h=H)
                sp.dma_start(dst, src.partition_broadcast(P)).then_inc(consts_in, 16)
            for i, src in enumerate((io["a_src"], io["a_dst"])):
                dst = sq[:, i, :].rearrange("p (h e) -> p h e", h=H)
                sp.dma_start(dst, src[:, 0, :].partition_broadcast(P)).then_inc(consts_in, 16)
            load_x(0, 0, 0)
            for k in range(CPB):
                transpose_chunk(0, k, 0)
            with sp.Fori(0, BPB) as p:
                for t in range(TPB):
                    load_x(p * TPB + t + 1, (t + 1) % 2, p * TPB + t)
                store_hu(p)

            def step(g, prep=False, last=False):
                for h in range(H):
                    if h == 0 and not last:
                        sp.wait_ge(unit_done, g * H)
                    stand(sp)
                    if not last:
                        for k in (2 * h, 2 * h + 1):
                            slot = k % A16_SLOTS
                            it, half = k // 2, k % 2
                            sp.wait_ge(a16_in[slot], (g * 2 + 2 + k // A16_SLOTS + 1) * 16)
                            stand(sp)
                            dst = mt[:, bass.ds((g + 1) % 2, 1), half * HALF:(half + 1) * HALF, it * P:(it + 1) * P]
                            sp.dma_start_transpose(dst.rearrange("p a j i -> p (a j) i"),
                                                   a16[:, slot, :]).then_inc(turned[slot], 16)
                    if prep:
                        tt = g * TPB + JT + h
                        load_x((tt + 1) % NT, (h + 1) % 2, tt)
                    if h == 0:
                        if not (isinstance(g, int) and g == 0):
                            sp.wait_ge(z_made, g - 1)
                        stand(sp)
                        load_residual(g)
                if prep:
                    store_hu(g + BPB)

            step(0, prep=True)
            with sp.Fori(1, NB - BPB) as g:
                step(g, prep=True)
            with sp.Fori(NB - BPB, NB - 1) as g:
                step(g)
            step(NB - 1, last=True)

        @block.gpsimd
        def _(pool):
            def load_chunk(g, k, ahead):
                slot = k % A16_SLOTS
                if ahead:
                    pool.wait_ge(turned[slot], (g * 2 + k // A16_SLOTS) * 16)
                    pool.wait_ge(adj_checked, g * CPB + k - A16_SLOTS + 1)
                stand(pool)
                src = adj_t[:, bass.ds(g * TPB + k // 2, 1), (k % 2) * CH:(k % 2) * CH + CH]
                pool.dma_start(a16[:, slot, :].unsqueeze(1), src).then_inc(a16_in[slot], 16)

            def weigh(t, slot):
                pool.wait_ge(hb_made, t + 1)
                pool.wait_ge(exps_made, t + 1)
                pool.wait_ge(vh_done, t)
                stand(pool)
                w = hu_out[:, slot, D:HC].rearrange("p (f s h) -> p f s h", f=2, s=2)[:, :, 1, :]
                for f in range(2):
                    pool.tensor_tensor(vh32[:, f, :, :], hb[:, :, :], tail_of(w[:, f, :], E1), ALU.mult)\
                        .then_inc(vh32_made, 1)

            def exps_of(g, h):
                e = hu_in[:, bass.ds(g % 2, 1), :, D:HC].rearrange("p a t c -> p (a t) c")
                return e.rearrange("p t (f s h) -> p f s h t", f=2, s=2)[:, :, 0, h, :]

            def denominator(g, h, u):
                pool.wait_ge(dens_read, u + 1)
                if h == 0:
                    pool.wait_ge(res_in, g * 32 + 32)
                stand(pool)
                ks = "p (k i) -> p k i"
                e = exps_of(g, h)
                pool.tensor_tensor(den_e[:], dens[:, :, :, 2], dens[:, :, :, 1], ALU.subtract).then_inc(den_step, 1)
                pool.tensor_tensor(den_m[:, 0, :, :], dens[:, :, :, 0], e[:, 0, :].rearrange(ks, k=2), ALU.mult)\
                    .then_inc(den_step, 1)
                pool.wait_ge(den_step, u * 3 + 2)
                stand(pool)
                pool.tensor_tensor(den_m[:, 1, :, :], den_e[:], e[:, 1, :].rearrange(ks, k=2), ALU.mult)\
                    .then_inc(den_step, 1)
                pool.wait_ge(den_step, u * 3 + 3)
                stand(pool)
                dst = met_den[:, bass.ds(u * TPB, TPB)].rearrange(ks, k=2)
                pool.tensor_tensor(dst, den_m[:, 0, :, :], den_m[:, 1, :, :], ALU.add).then_inc(den_made, 1)

            def weights(g, h, u):
                pool.wait_ge(rden_made, u + 1)
                pool.wait_ge(att_made, u)
                stand(pool)
                e = exps_of(g, h)
                pool.tensor_tensor(cw[:], e, rden[:].unsqueeze(1).to_broadcast([P, 2, TPB]), ALU.mult)\
                    .then_inc(cw_made, 1)

            def head_mean(g):
                pool.wait_ge(s1_made, g + 1)
                stand(pool)
                pool.tensor_scalar(m_head[:], s_head[:, 0, :], -1.0 / E, 0.0, ALU.mult, ALU.add).then_inc(mean_made, 1)

            def head_scale(g):
                pool.wait_ge(s2_made, g + 1)
                stand(pool)
                n = g * 5
                pool.tensor_scalar(s_head[:, 1, :], s_head[:, 1, :], 1.0 / E, EPS_HEAD, ALU.mult, ALU.add)\
                    .then_inc(norm_step, 1)
                pool.wait_ge(norm_step, n + 1)
                stand(pool)
                pool.tensor_tensor(r_head[:], s_head[:, 1, :], exponent[:], ALU.pow).then_inc(norm_step, 1)
                pool.wait_ge(norm_step, n + 2)
                stand(pool)
                a = att[:, bass.ds(g % 2, 1), :, :].rearrange("p a t d -> p (a t) d")
                ah = a.rearrange("p t (h e) -> p (t h) e", h=H)
                pool.tensor_tensor(ah, ah, tail_of(r_head[:], E), ALU.mult).then_inc(norm_step, 1)

            def head_gamma(g):
                n = g * 5
                a = att[:, bass.ds(g % 2, 1), :, :].rearrange("p a t d -> p (a t) d")
                pool.wait_ge(norm_step, n + 3)
                stand(pool)
                pool.tensor_tensor(a, a, gamma_bc[:].unsqueeze(1).to_broadcast([P, TPB, D]), ALU.mult)\
                    .then_inc(norm_step, 1)

            def head_beta(g):
                n = g * 5
                a = att[:, bass.ds(g % 2, 1), :, :].rearrange("p a t d -> p (a t) d")
                r = x_res[:, bass.ds(g % 2, 1), :, :].rearrange("p a t d -> p (a t) d")
                pool.wait_ge(norm_step, n + 4)
                stand(pool)
                pool.tensor_tensor(a, a, beta_bc[:].unsqueeze(1).to_broadcast([P, TPB, D]), ALU.add)\
                    .then_inc(norm_step, 1)
                pool.wait_ge(norm_step, n + 5)
                stand(pool)
                pool.tensor_tensor(a, a, r, ALU.add).then_inc(z_made, 1)

            def row_mean(g):
                pool.wait_ge(s3_made, g * TPB + TPB)
                stand(pool)
                pool.tensor_scalar(m_row[:], s_row[:, 0, :], -1.0 / D, 0.0, ALU.mult, ALU.add).then_inc(m2_made, 1)

            def row_scale(g):
                pool.wait_ge(s4_made, g * TPB + TPB)
                stand(pool)
                n = g * 3
                pool.tensor_scalar(s_row[:, 1, :], s_row[:, 1, :], 1.0 / D, EPS_ROW, ALU.mult, ALU.add)\
                    .then_inc(r2_made, 1)
                pool.wait_ge(r2_made, n + 1)
                stand(pool)
                pool.tensor_tensor(r_row[:], s_row[:, 1, :], exponent[:, 0:TPB], ALU.pow).then_inc(r2_made, 1)
                pool.wait_ge(r2_made, n + 2)
                stand(pool)
                pool.tensor_tensor(n_row[:], m_row[:], r_row[:], ALU.mult).then_inc(r2_made, 1)

            for k in range(A16_SLOTS):
                load_chunk(0, k, False)
            pool.wait_ge(consts_set, 6)
            stand(pool)
            for k in range(A16_SLOTS, CPB + A16_SLOTS):
                load_chunk(0, k, True)
            with pool.Fori(0, BPB) as p:
                for t in range(TPB):
                    weigh(p * TPB + t, t)

            def step(g, prep=False, first=False, last=False):
                for h in range(H):
                    u = g * H + h
                    before = (g, h - 1) if h else (g - 1, H - 1)
                    if not (first and h == 0):
                        denominator(*before, u - 1)
                    if prep:
                        weigh(u + JT, h)
                    if not (first and h == 0):
                        weights(*before, u - 1)
                    for k in (2 * h, 2 * h + 1):
                        if not last and not (isinstance(g, int) and g == NB - 2 and k >= A16_SLOTS):
                            load_chunk(g + 1, A16_SLOTS + k, True)
                    if not first:
                        if h == 1:
                            head_mean(g - 1)
                        if h == 2:
                            head_scale(g - 1)
                            head_gamma(g - 1)
                        if h == 3:
                            head_beta(g - 1)
                            row_mean(g - 1)
                            row_scale(g - 1)

            step(0, prep=True, first=True)
            with pool.Fori(1, NB - BPB) as g:
                step(g, prep=True)
            with pool.Fori(NB - BPB, NB - 2) as g:
                step(g)
            step(NB - 2)
            step(NB - 1, last=True)
            denominator(NB - 1, H - 1, NB * H - 1)
            weights(NB - 1, H - 1, NB * H - 1)
            head_mean(NB - 1)
            head_scale(NB - 1)
            head_gamma(NB - 1)
            head_beta(NB - 1)
            row_mean(NB - 1)
            row_scale(NB - 1)
            pool.wait_ge(met_done, 1)
            stand(pool)
            pool.partition_all_reduce(broken_all[:], broken[:, 4:5], P, RMAX).then_inc(viol_step, 1)
            pool.wait_ge(viol_step, 1)
            stand(pool)
            pool.tensor_copy(viol_i[:, :], broken_all[:]).then_inc(viol_step, 1)
            pool.wait_ge(viol_step, 2)
            stand(pool)

        @block.scalar
        def _(act):
            def copy_xT(t):
                act.wait_ge(x_turned, t + 1)
                act.wait_ge(h_made, t)
                stand(act)
                act.activation(xT[:, :, :], turn[:, 0:D].rearrange("p (k i) -> p k i", k=KD), ACT.Copy)\
                    .then_inc(xT_copied, 1)

            def projected(t, slot, stored=None):
                act.wait_ge(h_made, t + 1)
                if stored is not None:
                    act.wait_ge(hu_stored, stored)
                stand(act)
                act.activation(hu_out[:, slot, D:D + 2 * H], hp[:, D:D + 2 * H], ACT.Exp,
                               bias=ln_scale[:, 0:1])
                act.activation(hu_out[:, slot, D + 2 * H:HC], hp[:, D:D + 2 * H], ACT.Exp,
                               bias=ln_scale[:, 0:1], scale=LEAK).then_inc(exps_made, 1)
                act.wait_ge(h_read_act, t)
                stand(act)
                act.activation(scrap_e[:], hp[:, D:D + 2 * H], ACT.Square,
                               accum_out=met_exp[:, bass.ds(t, 1)])
                act.activation(hu_out[:, slot, 0:D], hp[:, 0:D], ACT.Copy).then_inc(h_read_act, 1)

            def high_parts(t):
                act.wait_ge(vh32_made, t * 2 + 2)
                act.wait_ge(vh_hi_done, t * 2)
                stand(act)
                act.activation(scrap_h[:], hb[:, :, :].rearrange("p h e -> p (h e)"), ACT.Square,
                               accum_out=met_h[:, bass.ds(t, 1)])
                for f in range(2):
                    dst = vh[:, bass.ds(batch_slot(t), 1), :, 0, f, :].rearrange("p a h e -> p (a h) e")
                    act.activation(dst, vh32[:, f, :, :], ACT.Copy).then_inc(vh_hi_done, 1)

            def na_high(p):
                act.wait_ge(na_turned, p + 1)
                stand(act)
                dst = na_t[:, bass.ds(p % NA_SLOTS, 1), 0, :].rearrange("p a i -> p (a i)")
                act.activation(dst, na_turn, ACT.Copy).then_inc(na_hi_done, 1)

            def check_chunk(g, k):
                slot = k % A16_SLOTS
                act.wait_ge(a16_in[slot], (g * 2 + k // A16_SLOTS + 1) * 16)
                if not (isinstance(g, int) and g == 0 and k < 2):
                    act.wait_ge(adj_checked, g * CPB + k - 1)
                stand(act)
                act.activation(scrap[:, k % 2, :], a16[:, slot, :], ACT.Square, bias=neg_half[:, 0:1],
                               accum_out=met_adj[:, bass.ds(g * CPB + k, 1)]).then_inc(adj_checked, 1)

            def read_sums(s, u):
                act.wait_ge(unit_done, u + 1)
                act.wait_ge(den_made, u)
                stand(act)
                act.activation(dens[:], regions(s, E, RW)[:, :, :, ::E1], ACT.Copy).then_inc(dens_read, 1)
                act.wait_ge(e2_made, u)
                stand(act)
                act.activation(m_sum[:], regions(s, 2 * E1, 2 * E1 + E), ACT.Copy).then_inc(m_read, 1)

            def first_terms(s, u):
                act.wait_ge(cw_made, u + 1)
                act.wait_ge(att_made, u)
                stand(act)
                for it in range(TPB):
                    act.activation(t1[:, it, :], region(s, it)[:, 0:E], ACT.Copy, scale=cw[:, 0, it:it + 1])\
                        .then_inc(t1_made, 1)

            def att_of(g):
                return att[:, bass.ds(g % 2, 1), :, :].rearrange("p a t d -> p (a t) d")

            def squares(g):
                act.wait_ge(cent_made, g + 1)
                stand(act)
                act.activation(sq[:], att_of(g), ACT.Square).then_inc(sq_made, 1)

            def row_sums(g):
                act.wait_ge(z_made, g + 1)
                stand(act)
                for it in range(TPB):
                    act.activation(sq[:, it, :], att_of(g)[:, it, :], ACT.Copy, accum_out=s_row[:, 0, it:it + 1])\
                        .then_inc(s3_made, 1)
                act.wait_ge(m2_made, g + 1)
                stand(act)
                for it in range(TPB):
                    act.activation(sq[:, it, :], att_of(g)[:, it, :], ACT.Square, bias=m_row[:, it:it + 1],
                                   accum_out=s_row[:, 1, it:it + 1]).then_inc(s4_made, 1)

            def finish_rows(g):
                act.wait_ge(r2_made, g * 3 + 3)
                act.wait_ge(out_stored, g * 16)
                stand(act)
                for it in range(TPB):
                    act.activation(fin[:, it, :], att_of(g)[:, it, :], ACT.Identity, bias=n_row[:, it:it + 1],
                                   scale=r_row[:, it:it + 1]).then_inc(fin_made, 1)
                act.wait_ge(fin_made, g * TPB + TPB)
                stand(act)
                act.dma_start(out_t[:, bass.ds(g * TPB, TPB), :], fin[:]).then_inc(out_stored, 16)

            act.wait_ge(consts_set, 6)
            stand(act)
            copy_xT(0)
            for k in range(CPB):
                check_chunk(0, k)
            with act.Fori(0, BPB) as p:
                for t in range(TPB):
                    tt = p * TPB + t
                    projected(tt, t, p * 16 if t == 0 else None)
                    high_parts(tt)
                    if t == TPB - 1:
                        na_high(p)
                    copy_xT(tt + 1)

            def step(g, prep=False, first=False, last=False):
                for h in range(H):
                    u = g * H + h
                    s_before = (h + 1) % 2
                    if not (first and h == 0):
                        read_sums(s_before, u - 1)
                    if prep:
                        projected(u + JT, h, (g + BPB) * 16 if h == 0 else None)
                        if h == 0:
                            act.wait_ge(unit_done, (g // BPB) * (H * BPB))
                        stand(act)
                        high_parts(u + JT)
                    if not (first and h == 0):
                        first_terms(s_before, u - 1)
                    if prep and h == H - 1:
                        na_high(g + BPB)
                    if not last:
                        check_chunk(g + 1, 2 * h)
                        check_chunk(g + 1, 2 * h + 1)
                    if prep:
                        copy_xT(u + JT + 1)
                    if not first:
                        if h == 1:
                            squares(g - 1)
                        if h == 3:
                            row_sums(g - 1)
                            finish_rows(g - 1)

            step(0, prep=True, first=True)
            with act.Fori(1, NB - BPB) as g:
                step(g, prep=True)
            with act.Fori(NB - BPB, NB - 1) as g:
                step(g)
            step(NB - 1, last=True)
            read_sums((NB * H - 1) % 2, NB * H - 1)
            first_terms((NB * H - 1) % 2, NB * H - 1)
            squares(NB - 1)
            row_sums(NB - 1)
            finish_rows(NB - 1)
            act.wait_ge(out_stored, NB * 16)
            stand(act)

        @block.vector
        def _(dve):
            def make_g(g, h, u, jt):
                b = bcol[:, bass.ds((g // BPB % 2) * JT + jt, 1), h]
                m = mt[:, bass.ds(g % 2, 1), jt, :].rearrange("p a i -> p (a i)")
                dve.scalar_tensor_tensor(out=g_sb[:, h % 2, jt, :], in0=na[:, h % 2, :], scalar=b, in1=m,
                                         op0=ALU.is_lt, op1=ALU.mult).then_inc(g_made, 1)

            def before_g(g, h, u):
                dve.wait_ge(na_made, u + 1)
                if not (isinstance(u, int) and u < 2):
                    dve.wait_ge(unit_done, u - 1)
                if h == 0:
                    dve.wait_ge(h_read_dve, (g // BPB + 1) * JT)
                    for slot in range(A16_SLOTS):
                        dve.wait_ge(turned[slot], (g + 1) * (CPB // A16_SLOTS) * 16)

            def add_bias(t, slot):
                dve.wait_ge(h_read_act, t + 1)
                dve.wait_ge(vh_hi_done, t * 2)
                dve.wait_ge(vh32_made, t * 2)
                dst = hb[:, :, 0:E]
                src = hp[:, 0:D].rearrange("p (h e) -> p h e", h=H)
                dve.tensor_tensor(dst, src, bias_bc[:].rearrange("p (h e) -> p h e", h=H), ALU.add).then_inc(hb_made, 1)
                if slot == 0:
                    pass
                dve.tensor_scalar(na_c[:, :, slot], hp[:, D:D + H], -1.0, None, ALU.mult)
                dst = bcol[:, bass.ds(batch_slot(t), 1), :].rearrange("p a h -> p (a h)")
                dve.tensor_copy(dst, hp[:, D + H:D + 2 * H]).then_inc(h_read_dve, 1)

            def low_parts(t):
                dve.wait_ge(vh_hi_done, t * 2 + 2)
                for f in range(2):
                    v = vh[:, bass.ds(batch_slot(t), 1), :, :, f, :].rearrange("p a h s e -> p (a h) s e")
                    ins = dve.tensor_tensor(v[:, :, 1, :], vh32[:, f, :, :], v[:, :, 0, :], ALU.subtract)
                ins.then_inc(vh_done, 1)

            def na_low(p):
                dve.wait_ge(na_hi_done, p + 1)
                n = na_t[:, bass.ds(p % NA_SLOTS, 1), :, :].rearrange("p a s i -> p (a s) i")
                dve.tensor_tensor(n[:, 1, :], na_turn, n[:, 0, :], ALU.subtract).then_inc(na_split, 1)

            def reciprocals(u):
                dve.wait_ge(den_made, u + 1)
                dve.wait_ge(cw_made, u)
                dve.tensor_scalar(rden_in[:], met_den[:, bass.ds(u * TPB, TPB)], DEN_LEAST, None, ALU.max)                    .then_inc(rden_safe, 1)
                dve.wait_ge(rden_safe, u + 1)
                dve.reciprocal(rden[:], rden_in[:]).then_inc(rden_made, 1)

            def second_terms(g, h, u, s):
                dve.wait_ge(m_read, u + 1)
                dve.wait_ge(t1_made, u * TPB + TPB)
                e = e2[:].rearrange("p (k i) e -> p k i e", k=2)
                dve.tensor_tensor(e, m_sum[:], regions(s, E1, E1 + E), ALU.subtract).then_inc(e2_made, 1)
                dve.wait_ge(e2_made, u + 1)
                if h == 0 and not (isinstance(g, int) and g < 2):
                    dve.wait_ge(fin_made, (g - 1) * TPB)
                for it in range(TPB):
                    dst = att[:, bass.ds(g % 2, 1), it, h * E:(h + 1) * E].rearrange("p a e -> p (a e)")
                    ins = dve.scalar_tensor_tensor(out=dst, in0=e2[:, it, :], scalar=cw[:, 1, it:it + 1],
                                                   in1=t1[:, it, :], op0=ALU.mult, op1=ALU.add)
                ins.then_inc(att_made, 1)

            def att_of(g):
                return att[:, bass.ds(g % 2, 1), :, :].rearrange("p a t d -> p (a t) d")

            def residual(g):
                dve.wait_ge(att_made, g * H + H)
                dve.wait_ge(res_in, g * 32 + 32)
                hh = hu_in[:, bass.ds(g % 2, 1), :, 0:D].rearrange("p a t d -> p (a t) d")
                dve.scalar_tensor_tensor(out=att_of(g), in0=att_of(g), scalar=0.0, in1=hh,
                                         op0=ALU.max, op1=ALU.add).then_inc(o_made, 1)
                dve.wait_ge(mean_made, g)
                dve.wait_ge(o_made, g + 1)
                stand(dve)
                dve.reduce_sum(s_head[:, 0, :], att_of(g).rearrange("p t (h e) -> p (t h) e", h=H), AX.X)\
                    .then_inc(s1_made, 1)

            def centre(g):
                dve.wait_ge(mean_made, g + 1)
                ah = att_of(g).rearrange("p t (h e) -> p (t h) e", h=H)
                dve.tensor_tensor(ah, ah, tail_of(m_head[:], E), ALU.add).then_inc(cent_made, 1)

            def square_sums(g):
                dve.wait_ge(sq_made, g + 1)
                dve.wait_ge(norm_step, g * 5)
                stand(dve)
                dve.reduce_sum(s_head[:, 1, :], sq[:].rearrange("p t (h e) -> p (t h) e", h=H), AX.X)\
                    .then_inc(s2_made, 1)

            dve.memset(neg_half[:], -0.5).then_inc(consts_set, 1)
            dve.memset(ln_scale[:], LN_V_SCALE).then_inc(consts_set, 1)
            dve.memset(exponent[:], -0.5).then_inc(consts_set, 1)
            dve.memset(hb[:], 1.0).then_inc(consts_set, 1)
            dve.wait_ge(consts_in, 16 * (1 + KD + 5))
            dve.tensor_copy(sel[:], tail_of(ident[0:TPB * H, 0:TPB * H], P)).then_inc(consts_set, 1)
            n = 0
            for k in range(KD):
                for i in range(2):
                    prod = fin[:, 2 * k + i, :].rearrange("p (h e) -> p h e", h=H)
                    a = sq[:, i, :].rearrange("p (h e) -> p h e", h=H)
                    dve.tensor_tensor(prod, wa[:, k, 0:D].rearrange("p (h e) -> p h e", h=H), a, ALU.mult)\
                        .then_inc(wa_done, 1)
            dve.wait_ge(wa_done, 2 * KD)
            for k in range(KD):
                for i in range(2):
                    prod = fin[:, 2 * k + i, :].rearrange("p (h e) -> p h e", h=H)
                    ins = dve.reduce_sum(wa[:, k, D + i * H:D + (i + 1) * H], prod, AX.X)
            ins.then_inc(consts_set, 1)
            dve.wait_ge(consts_set, 6)

            with dve.Fori(0, BPB) as p:
                for t in range(TPB):
                    add_bias(p * TPB + t, t)
                    low_parts(p * TPB + t)
                na_low(p)
            before_g(0, 0, 0)
            for jt in range(JT):
                make_g(0, 0, 0, jt)

            def step(g, prep=False, first=False, last=False):
                for h in range(H):
                    u = g * H + h
                    after = (g, h + 1) if h + 1 < H else (g + 1, 0)
                    before = (g, h - 1) if h else (g - 1, H - 1)
                    g_too = not (last and h == H - 1)
                    result = not (first and h == 0)
                    if prep and h == H - 1:
                        add_bias(u + JT, h)
                    if g_too:
                        before_g(*after, u + 1)
                    for jt in range(JT):
                        if g_too:
                            make_g(*after, u + 1, jt)
                        if jt == 2 and prep and h < H - 1:
                            add_bias(u + JT, h)
                        if jt == 8 and result:
                            reciprocals(u - 1)
                        if jt == 10 and prep:
                            low_parts(u + JT)
                        if jt == 12 and prep and h == H - 1:
                            na_low(g + BPB)
                        if jt == 14 and result:
                            second_terms(*before, u - 1, (h + 1) % 2)
                        if not first and h == 1:
                            if jt == 3:
                                residual(g - 1)
                            if jt == 11:
                                centre(g - 1)
                        if not first and h == 2 and jt == 3:
                            square_sums(g - 1)

            step(0, prep=True, first=True)
            with dve.Fori(1, NB - BPB) as g:
                step(g, prep=True)
            with dve.Fori(NB - BPB, NB - 1) as g:
                step(g)
            step(NB - 1, last=True)
            u = NB * H - 1
            reciprocals(u)
            second_terms(NB - 1, H - 1, u, u % 2)
            residual(NB - 1)
            centre(NB - 1)
            square_sums(NB - 1)
            dve.wait_ge(adj_checked, NB * CPB)
            dve.wait_ge(vh_hi_done, NT * 2)
            for i, (met, op) in enumerate(((met_adj, ALU.max), (met_exp, ALU.max), (met_h, ALU.max), (met_den, ALU.min))):
                dve.tensor_reduce(worst[:, i:i + 1], met[:], AX.X, op).then_inc(viol_step_dve, 1)
            dve.wait_ge(viol_step_dve, 4)
            for i, (most, op) in enumerate(((CH / 4.0, ALU.is_gt), (EXP_SQ, ALU.is_gt), (H_SQ, ALU.is_gt), (DEN_LEAST, ALU.is_lt))):
                dve.tensor_scalar(broken[:, i:i + 1], worst[:, i:i + 1], most, None, op).then_inc(viol_step_dve, 1)
            dve.wait_ge(viol_step_dve, 8)
            dve.tensor_reduce(broken[:, 4:5], broken[:, 0:4], AX.X, ALU.max).then_inc(met_done, 1)

        @block.tensor
        def _(pe):
            def turn_x(t, slot):
                pe.wait_ge(x_in[slot], (t // 2) * 16 + 16)
                pe.wait_ge(xT_copied, t)
                for k in range(KD):
                    ins = pe.transpose(turn[:, k * P:(k + 1) * P], xin[:, slot, k * P:(k + 1) * P], ident[:])
                ins.then_inc(x_turned, 1)

            def project(t, t_of_block, blocks_turned):
                pe.wait_ge(xT_copied, t + 1)
                pe.wait_ge(h_read_dve, t)
                if t_of_block == 0:
                    pe.wait_ge(na_split, blocks_turned)
                for k in range(KD):
                    ins = pe.matmul(hp[:, 0:D + 2 * H], xT[:, k, :], wa[:, k, :], start=(k == 0), stop=(k == KD - 1))
                ins.then_inc(h_made, 1)

            def turn_na(p):
                pe.wait_ge(h_read_dve, p * TPB + TPB)
                pe.transpose(na_turn, na_c[:].rearrange("p h t -> p (h t)"), ident[:]).then_inc(na_turned, 1)

            def spread_na(g, h, u):
                if isinstance(u, int) and u < 2:
                    pass
                else:
                    pe.wait_ge(g_made, (u - 1) * JT)
                if h == 0:
                    pe.wait_ge(na_split, g + 1)
                stand(pe)
                for it in range(TPB):
                    for s in range(2):
                        rhs = na_t[:, bass.ds(g % NA_SLOTS, 1), s, :].rearrange("p a i -> p (a i)")
                        ins = pe.matmul(na[:, h % 2, it * P:(it + 1) * P], sel[:, h * TPB + it, :], rhs,
                                        start=(s == 0), stop=(s == 1))
                ins.then_inc(na_made, 1)

            def sums(batch_half, g_half, h, u, it):
                s = h % 2
                out = region(s, it)
                for jt in range(JT):
                    if it == 0 and jt % 4 == 0:
                        pe.wait_ge(g_made, u * JT + jt + 4)
                    v = vh[:, batch_half * JT + jt, h, :, :, :]
                    gg = g_sb[:, s, jt, it * P:(it + 1) * P]
                    mm = mt[:, g_half, jt, it * P:(it + 1) * P]
                    for part in range(2):
                        pe.matmul(out[:, 0:2 * E1], gg, v[:, part, :, :].rearrange("p f e -> p (f e)"),
                                  start=(jt == 0 and part == 0), stop=False, skip_group_check=True)
                    for part in range(2):
                        ins = pe.matmul(out[:, 2 * E1:RW], mm, v[:, part, 1, :], start=False,
                                        stop=(jt == JT - 1 and part == 1), skip_group_check=True)
                return ins

            pe.wait_ge(consts_set, 6)
            turn_x(0, 0)
            with pe.Fori(0, BPB) as p:
                for t in range(TPB):
                    tt = p * TPB + t
                    project(tt, t, p)
                    if t == TPB - 1:
                        turn_na(p)
                    turn_x(tt + 1, (t + 1) % 2)
            spread_na(0, 0, 0)
            spread_na(0, 1, 1)

            def step(g, batch_half, prep=False, last=False):
                for k in range(2 * H):
                    h, g_half = k % H, k // H
                    u = g * H + k
                    if prep:
                        project(u + JT, h, g + g_half + BPB)
                    if not (last and k >= 2 * H - 2):
                        spread_na(g + (k + 2) // H, (k + 2) % H, u + 2)
                    if k == 0:
                        pe.wait_ge(vh_done, (g // BPB + 1) * JT)
                    for it in range(TPB):
                        ins = sums(batch_half, g_half, h, u, it)
                        if it == 0 and prep and h == H - 1:
                            turn_na(g + g_half + BPB)
                        if it == 1 and prep:
                            turn_x(u + JT + 1, (h + 1) % 2)
                    ins.then_inc(unit_done, 1)
                    pe.wait_ge(att_made, u)

            if B > 2:
                with pe.Fori(0, B // 2 - 1) as pair:
                    for half in range(2):
                        with pe.Fori(0, BPB // 2) as q:
                            step(pair * (2 * BPB) + q * 2 + half * BPB, half, prep=True)
            with pe.Fori(0, BPB // 2) as q:
                step(q * 2 + NB - 2 * BPB, 0, prep=True)
            with pe.Fori(0, BPB // 2 - 1) as q:
                step(q * 2 + NB - BPB, 1)
            step(NB - 2, 1, last=True)


def general_path(nc, io, viol_i, sems):
    x, adj, W = io["x"], io["adj"], io["W"]
    B, N, D, H, E = dims(x, adj, W)
    T = io["a_src"].shape[1]
    JT = N // P
    NT = B * JT
    KD = D // P
    HT = H * T
    PC = D + HT
    CW = min(512, N)
    CK = N // CW
    NEG = -1e9

    x_t = x.rearrange("b (t p) d -> p (b t) d", p=P)
    out_t = io["out"].rearrange("b (t p) d -> p (b t) d", p=P)
    adj_t = adj.rearrange("b (t p) n -> p (b t) n", p=P)
    heads_t = io["hu"][:, 0:D].rearrange("(t p) c -> p t c", p=P)

    with ExitStack() as ctx:
        def sb(name, shape, dt=F32):
            return ctx.enter_context(nc.sbuf_tensor(name, shape, dt))

        def psum(name, shape, dt=F32):
            return ctx.enter_context(nc.psum_tensor(name, shape, dt))

        def sem(name):
            return sems.enter_context(nc.semaphore(name))

        ident = sb("g_ident", [P, P])
        wp = sb("g_wp", [P, KD, PC])
        wd = sb("g_wd", [P, KD, HT])
        wd_rep = sb("g_wd_rep", [P, KD, T, P])
        a_bc = sb("g_a_bc", [P, 2, HT, E])
        prod = sb("g_prod", [P, HT, E])
        bias_bc = sb("g_bias", [P, D])
        gamma_bc = sb("g_gamma", [P, D])
        beta_bc = sb("g_beta", [P, D])
        half_neg = sb("g_half_neg", [P, 1])
        xin = sb("g_xin", [P, D])
        xT = sb("g_xT", [P, KD, N])
        xT_tile = sb("g_xT_tile", [P, KD, P])
        hs = sb("g_h", [P, JT, PC])
        b_bc = sb("g_b_bc", [P, T, N])
        adj_i = sb("g_adj_i", [P, N], I32)
        adj_f = sb("g_adj_f", [P, N])
        mask = sb("g_mask", [P, N])
        w = sb("g_w", [P, N])
        term = sb("g_term", [P, N])
        pr = sb("g_p", [P, N])
        prT = sb("g_pT", [P, JT, P])
        st = sb("g_st", [P, 12])
        o = sb("g_o", [P, E])
        c = sb("g_c", [P, E])
        z = sb("g_z", [P, D])
        zc = sb("g_zc", [P, D])
        xr = sb("g_xr", [P, D])

        ps_x = psum("g_ps_x", [P, 512])
        ps_h = psum("g_ps_h", [P, 512])
        ps_b = psum("g_ps_b", [P, 512])
        ps_p = psum("g_ps_p", [P, 512])
        ps_o = psum("g_ps_o", [P, 512])

        consts_in = sem("g_consts_in")
        consts_set = sem("g_consts_set")
        x_in = sem("g_x_in")
        x_turned = sem("g_x_turned")
        xT_copied = sem("g_xT_copied")
        h_made = sem("g_h_made")
        h_copied = sem("g_h_copied")
        rep_made = sem("g_rep_made")
        b_made = sem("g_b_made")
        b_copied = sem("g_b_copied")
        adj_in = sem("g_adj_in")
        adj_read = sem("g_adj_read")
        dve_step = sem("g_dve_step")
        w_made = sem("g_w_made")
        p_made = sem("g_p_made")
        p_turned = sem("g_p_turned")
        pT_copied = sem("g_pT_copied")
        sum_made = sem("g_sum_made")
        var_made = sem("g_var_made")
        std_made = sem("g_std_made")
        head_made = sem("g_head_made")
        head_stored = sem("g_head_stored")
        z_in = sem("g_z_in")
        row_var = sem("g_row_var")
        row_std = sem("g_row_std")
        row_scaled = sem("g_row_scaled")
        row_made = sem("g_row_made")
        row_stored = sem("g_row_stored")
        stood = {e.engine: sem(f"g_stood_{n}") for n, e in
                 (("sp", nc.sync), ("pool", nc.gpsimd), ("act", nc.scalar), ("dve", nc.vector), ("pe", nc.tensor))}

        def stand(eng):
            eng.sem_inc(stood[eng.engine], 1)

        block = ctx.enter_context(nc.Block())
        TILE_STEPS = 3 * T + 13

        @block.sync
        def _(sp):
            with sp.If(sp.value_load(viol_i[0:1, 0:1], min_val=0, max_val=1) > 0):
                sp.dma_start(ident[:], io["eye"]).then_inc(consts_in, 16)
                for k in range(KD):
                    dst = wp[:, k, 0:D].rearrange("p (h e) -> p h e", h=H)
                    sp.dma_start(dst, W.rearrange("h (k p) e -> k p h e", p=P)[k]).then_inc(consts_in, 16)
                for tile, src in ((bias_bc, io["bias"]), (gamma_bc, io["gamma"]), (beta_bc, io["beta"])):
                    dst = tile[:].rearrange("p (h e) -> p h e", h=H)
                    sp.dma_start(dst, src.partition_broadcast(P)).then_inc(consts_in, 16)
                for i, src in enumerate((io["a_src"], io["a_dst"])):
                    sp.dma_start(a_bc[:, i, :, :], src.rearrange("h t e -> (h t) e").partition_broadcast(P))\
                        .then_inc(consts_in, 16)
                with sp.Fori(0, B) as b:
                    with sp.Fori(0, JT) as t:
                        sp.wait_ge(x_turned, b * JT + t)
                        stand(sp)
                        sp.dma_start(xin[:].unsqueeze(1), x_t[:, bass.ds(b * JT + t, 1), :]).then_inc(x_in, 16)
                    with sp.Fori(0, H) as h:
                        with sp.Fori(0, JT) as t:
                            n = (b * H + h) * JT + t
                            sp.wait_ge(adj_read, n)
                            stand(sp)
                            sp.dma_start(adj_i[:].unsqueeze(1), adj_t[:, bass.ds(b * JT + t, 1), :])\
                                .then_inc(adj_in, 16)
                            sp.wait_ge(head_made, n + 1)
                            stand(sp)
                            dst = heads_t[:, bass.ds(b * JT + t, 1), bass.ds(h * E, E)]
                            sp.dma_start(dst, o[:].unsqueeze(1)).then_inc(head_stored, 16)
                sp.wait_ge(head_stored, B * H * JT * 16)
                with sp.Fori(0, NT) as t:
                    sp.wait_ge(row_made, t)
                    stand(sp)
                    sp.dma_start(z[:].unsqueeze(1), heads_t[:, bass.ds(t, 1), :]).then_inc(z_in, 16)
                    sp.dma_start(xr[:].unsqueeze(1), x_t[:, bass.ds(t, 1), :]).then_inc(z_in, 16)
                    sp.wait_ge(row_made, t + 1)
                    stand(sp)
                    sp.dma_start(out_t[:, bass.ds(t, 1), :], zc[:].unsqueeze(1)).then_inc(row_stored, 16)
                sp.wait_ge(row_stored, NT * 16)

        @block.tensor
        def _(pe):
            with pe.If(pe.value_load(viol_i[0:1, 0:1], min_val=0, max_val=1) > 0):
                pe.wait_ge(consts_set, 2)
                pe.wait_ge(consts_in, 16 * (KD + 6))
                with pe.Fori(0, B) as b:
                    with pe.Fori(0, JT) as t:
                        n = b * JT + t
                        pe.wait_ge(x_in, n * 16 + 16)
                        pe.wait_ge(xT_copied, n * 2)
                        stand(pe)
                        for k in range(KD):
                            ins = pe.transpose(ps_x[:, k * P:(k + 1) * P], xin[:, k * P:(k + 1) * P], ident[:])
                        ins.then_inc(x_turned, 1)
                        pe.wait_ge(xT_copied, n * 2 + 2)
                        pe.wait_ge(h_copied, n)
                        stand(pe)
                        for k in range(KD):
                            ins = pe.matmul(ps_h[:, 0:PC], xT_tile[:, k, :], wp[:, k, :],
                                            start=(k == 0), stop=(k == KD - 1))
                        ins.then_inc(h_made, 1)
                    with pe.Fori(0, H) as h:
                        pe.wait_ge(rep_made, b * H + h + 1)
                        pe.wait_ge(xT_copied, (b * JT + JT) * 2)
                        stand(pe)
                        for q in range(T * CK):
                            ty, ch = q // CK, q % CK
                            pe.wait_ge(b_copied, (b * H + h) * (T * CK) + q)
                            stand(pe)
                            for k in range(KD):
                                ins = pe.matmul(ps_b[:, 0:CW], wd_rep[:, k, ty, :], xT[:, k, ch * CW:(ch + 1) * CW],
                                                start=(k == 0), stop=(k == KD - 1))
                            ins.then_inc(b_made, 1)
                        with pe.Fori(0, JT) as t:
                            n = (b * H + h) * JT + t
                            pe.wait_ge(p_made, n + 1)
                            pe.wait_ge(h_copied, b * JT + JT)
                            stand(pe)
                            for ch in range(CK):
                                pe.wait_ge(pT_copied, n * CK + ch)
                                stand(pe)
                                for q in range(CW // P):
                                    j = ch * (CW // P) + q
                                    ins = pe.transpose(ps_p[:, q * P:(q + 1) * P], pr[:, j * P:(j + 1) * P], ident[:])
                                ins.then_inc(p_turned, 1)
                            pe.wait_ge(pT_copied, n * CK + CK)
                            pe.wait_ge(head_made, n)
                            stand(pe)
                            for j in range(JT):
                                ins = pe.matmul(ps_o[:, 0:E], prT[:, j, :], hs[:, j, bass.ds(h * E, E)],
                                                start=(j == 0), stop=(j == JT - 1))
                            ins.then_inc(sum_made, 1)

        @block.scalar
        def _(act):
            with act.If(act.value_load(viol_i[0:1, 0:1], min_val=0, max_val=1) > 0):
                with act.Fori(0, B) as b:
                    with act.Fori(0, JT) as t:
                        n = b * JT + t
                        act.wait_ge(x_turned, n + 1)
                        act.wait_ge(b_made, b * H * T * CK)
                        stand(act)
                        turned = ps_x[:, 0:D].rearrange("p (k i) -> p k i", k=KD)
                        act.activation(xT[:, :, bass.ds(t * P, P)], turned, ACT.Copy).then_inc(xT_copied, 1)
                        act.activation(xT_tile[:], turned, ACT.Copy).then_inc(xT_copied, 1)
                        act.wait_ge(h_made, n + 1)
                        act.wait_ge(head_made, b * H * JT)
                        stand(act)
                        act.activation(hs[:, bass.ds(t, 1), :].rearrange("p a c -> p (a c)"), ps_h[:, 0:PC], ACT.Copy)\
                            .then_inc(h_copied, 1)
                    with act.Fori(0, H) as h:
                        act.wait_ge(w_made, (b * H + h) * JT)
                        stand(act)
                        for q in range(T * CK):
                            ty, ch = q // CK, q % CK
                            act.wait_ge(b_made, (b * H + h) * (T * CK) + q + 1)
                            stand(act)
                            act.activation(b_bc[:, ty, ch * CW:(ch + 1) * CW], ps_b[:, 0:CW], ACT.Copy)\
                                .then_inc(b_copied, 1)
                        with act.Fori(0, JT) as t:
                            n = (b * H + h) * JT + t
                            act.wait_ge(w_made, n + 1)
                            act.wait_ge(p_turned, n * CK)
                            act.wait_ge(head_made, n)
                            stand(act)
                            act.activation(pr[:], w[:], ACT.Exp, bias=st[:, 0:1], accum_out=st[:, 1:2]).then_inc(p_made, 1)
                            for ch in range(CK):
                                act.wait_ge(p_turned, n * CK + ch + 1)
                                act.wait_ge(sum_made, n)
                                stand(act)
                                dst = prT[:, ch * (CW // P):(ch + 1) * (CW // P), :]
                                act.activation(dst, ps_p[:, 0:CW].rearrange("p (q i) -> p q i", i=P), ACT.Copy)\
                                    .then_inc(pT_copied, 1)

        @block.vector
        def _(dve):
            with dve.If(dve.value_load(viol_i[0:1, 0:1], min_val=0, max_val=1) > 0):
                dve.memset(half_neg[:], -0.5).then_inc(consts_set, 1)
                dve.wait_ge(consts_in, 16 * (KD + 6))
                n = 0
                for i, dst in enumerate((wp, wd)):
                    for k in range(KD):
                        for h in range(H):
                            wk = wp[:, k, h * E:(h + 1) * E].unsqueeze(1).to_broadcast([P, T, E])
                            if n:
                                dve.wait_ge(dve_step, n)
                            dve.tensor_tensor(prod[:, 0:T, :], wk, a_bc[:, i, h * T:(h + 1) * T, :], ALU.mult)\
                                .then_inc(dve_step, 1)
                            dve.wait_ge(dve_step, n + 1)
                            off = (D if i == 0 else 0) + h * T
                            dve.reduce_sum(dst[:, k, off:off + T], prod[:, 0:T, :], AX.X).then_inc(dve_step, 1)
                            n += 2
                dve.wait_ge(dve_step, n)
                dve.memset(c[:], 0.0).then_inc(consts_set, 1)
                first = n
                with dve.Fori(0, B) as b:
                    with dve.Fori(0, H) as h:
                        dve.wait_ge(b_made, (b * H + h) * (T * CK))
                        stand(dve)
                        src = wd[:, :, bass.ds(h * T, T)]
                        for k in range(KD):
                            ins = dve.tensor_copy(wd_rep[:, k, :, :], src[:, k, :].unsqueeze(2).to_broadcast([P, T, P]))
                        ins.then_inc(rep_made, 1)
                        dve.wait_ge(b_copied, (b * H + h + 1) * (T * CK))
                        dve.wait_ge(h_copied, b * JT + JT)
                        stand(dve)
                        with dve.Fori(0, JT) as t:
                            m = (b * H + h) * JT + t
                            s0 = m * TILE_STEPS + first

                            def done(i):
                                dve.wait_ge(dve_step, s0 + i)
                                stand(dve)

                            dve.wait_ge(adj_in, m * 16 + 16)
                            dve.wait_ge(p_made, m)
                            stand(dve)
                            dve.tensor_copy(adj_f[:], adj_i[:]).then_inc(adj_read, 1)
                            dve.wait_ge(adj_read, m + 1)
                            stand(dve)
                            dve.tensor_scalar(w[:], adj_f[:], 0.0, 0.0, ALU.mult, ALU.mult).then_inc(dve_step, 1)
                            for ty in range(T):
                                done(3 * ty + 1)
                                dve.tensor_scalar(mask[:], adj_f[:], float(ty + 1), None, ALU.is_equal)\
                                    .then_inc(dve_step, 1)
                                done(3 * ty + 2)
                                a = hs[:, bass.ds(t, 1), bass.ds(h * T + (D + ty), 1)].rearrange("p a c -> p (a c)")
                                dve.scalar_tensor_tensor(out=term[:], in0=b_bc[:, ty, :], scalar=a, in1=mask[:],
                                                         op0=ALU.add, op1=ALU.mult).then_inc(dve_step, 1)
                                done(3 * ty + 3)
                                dve.tensor_tensor(w[:], w[:], term[:], ALU.add).then_inc(dve_step, 1)
                            done(3 * T + 1)
                            dve.scalar_tensor_tensor(out=term[:], in0=w[:], scalar=LEAK, in1=w[:],
                                                     op0=ALU.mult, op1=ALU.max).then_inc(dve_step, 1)
                            dve.tensor_scalar(mask[:], adj_f[:], 0.0, NEG, ALU.is_equal, ALU.mult).then_inc(dve_step, 1)
                            done(3 * T + 3)
                            dve.tensor_tensor(w[:], term[:], mask[:], ALU.add).then_inc(dve_step, 1)
                            done(3 * T + 4)
                            dve.tensor_reduce(st[:, 2:3], w[:], AX.X, ALU.max).then_inc(dve_step, 1)
                            done(3 * T + 5)
                            dve.tensor_scalar(st[:, 0:1], st[:, 2:3], -1.0, None, ALU.mult).then_inc(w_made, 1)
                            dve.wait_ge(p_made, m + 1)
                            dve.wait_ge(sum_made, m + 1)
                            dve.wait_ge(head_stored, m * 16)
                            stand(dve)
                            dve.reciprocal(st[:, 3:4], st[:, 1:2]).then_inc(dve_step, 1)
                            done(3 * T + 6)
                            hb = bass.ds(h * E, E)
                            dve.scalar_tensor_tensor(out=o[:], in0=ps_o[:, 0:E], scalar=st[:, 3:4],
                                                     in1=bias_bc[:, hb], op0=ALU.mult, op1=ALU.add).then_inc(dve_step, 1)
                            done(3 * T + 7)
                            hh = hs[:, bass.ds(t, 1), hb].rearrange("p a e -> p (a e)")
                            dve.scalar_tensor_tensor(out=c[:], in0=o[:], scalar=0.0, in1=hh,
                                                     op0=ALU.max, op1=ALU.add).then_inc(dve_step, 1)
                            done(3 * T + 8)
                            dve.reduce_sum(st[:, 4:5], c[:], AX.X).then_inc(dve_step, 1)
                            done(3 * T + 9)
                            dve.tensor_scalar(st[:, 5:6], st[:, 4:5], -1.0 / E, None, ALU.mult).then_inc(dve_step, 1)
                            done(3 * T + 10)
                            dve.tensor_scalar(c[:], c[:], st[:, 5:6], None, ALU.add).then_inc(dve_step, 1)
                            done(3 * T + 11)
                            dve.tensor_tensor(o[:], c[:], c[:], ALU.mult).then_inc(dve_step, 1)
                            done(3 * T + 12)
                            dve.reduce_sum(st[:, 6:7], o[:], AX.X).then_inc(dve_step, 1)
                            done(3 * T + 13)
                            dve.tensor_scalar(st[:, 7:8], st[:, 6:7], 1.0 / E, EPS_HEAD, ALU.mult, ALU.add)\
                                .then_inc(var_made, 1)
                            dve.wait_ge(std_made, m + 1)
                            stand(dve)
                            dve.scalar_tensor_tensor(out=o[:], in0=c[:], scalar=st[:, 8:9], in1=gamma_bc[:, hb],
                                                     op0=ALU.mult, op1=ALU.mult).then_inc(var_made, 1)
                            dve.wait_ge(var_made, m * 2 + 2)
                            stand(dve)
                            dve.tensor_tensor(o[:], o[:], beta_bc[:, hb], ALU.add).then_inc(head_made, 1)
                with dve.Fori(0, NT) as t:
                    def done_row(i):
                        dve.wait_ge(row_var, t * 6 + i)
                        stand(dve)

                    dve.wait_ge(z_in, t * 32 + 32)
                    stand(dve)
                    dve.tensor_tensor(z[:], z[:], xr[:], ALU.add).then_inc(row_var, 1)
                    done_row(1)
                    dve.reduce_sum(st[:, 9:10], z[:], AX.X).then_inc(row_var, 1)
                    done_row(2)
                    dve.tensor_scalar(st[:, 10:11], st[:, 9:10], -1.0 / D, None, ALU.mult).then_inc(row_var, 1)
                    dve.wait_ge(row_stored, t * 16)
                    done_row(3)
                    dve.tensor_scalar(z[:], z[:], st[:, 10:11], None, ALU.add).then_inc(row_var, 1)
                    done_row(4)
                    dve.tensor_tensor(zc[:], z[:], z[:], ALU.mult).then_inc(row_var, 1)
                    done_row(5)
                    dve.reduce_sum(st[:, 9:10], zc[:], AX.X).then_inc(row_var, 1)
                    dve.wait_ge(row_std, t + 1)
                    stand(dve)
                    dve.tensor_scalar(zc[:], z[:], st[:, 11:12], None, ALU.mult).then_inc(row_made, 1)

        @block.gpsimd
        def _(pool):
            with pool.If(pool.value_load(viol_i[0:1, 0:1], min_val=0, max_val=1) > 0):
                pool.wait_ge(consts_set, 1)
                with pool.Fori(0, B * H * JT) as m:
                    pool.wait_ge(var_made, m * 2 + 1)
                    stand(pool)
                    pool.tensor_tensor(st[:, 8:9], st[:, 7:8], half_neg[:], ALU.pow).then_inc(std_made, 1)
                with pool.Fori(0, NT) as t:
                    pool.wait_ge(row_var, t * 6 + 6)
                    stand(pool)
                    pool.tensor_scalar(st[:, 7:8], st[:, 9:10], 1.0 / D, EPS_ROW, ALU.mult, ALU.add)\
                        .then_inc(row_scaled, 1)
                    pool.wait_ge(row_scaled, t + 1)
                    stand(pool)
                    pool.tensor_tensor(st[:, 11:12], st[:, 7:8], half_neg[:], ALU.pow).then_inc(row_std, 1)




_SHORT = {"x": "x", "adj": "adj", "L0_gnn_W": "W", "L0_gnn_a_src": "a_src", "L0_gnn_a_dst": "a_dst",
          "L0_gnn_bias": "bias", "L0_gnn_ln_gamma": "gamma", "L0_gnn_ln_beta": "beta"}


def gat_layer(nc, io):
    with nc.sbuf_tensor("viol_i", [P, 1], I32) as viol_i, ExitStack() as sems:
        main_path(nc, io, viol_i, sems)
        general_path(nc, io, viol_i, sems)


def kernel(**inputs):
    import numpy as np
    import concourse.bacc as bacc
    from concourse.bass_utils import run_bass_kernel_spmd

    nc = bacc.Bacc("TRN2", target_bir_lowering=False, num_devices=1)
    arrays, io = {}, {}
    for name, short in _SHORT.items():
        a = np.ascontiguousarray(inputs[name])
        arrays[f"in_{short}"] = a
        io[short] = nc.dram_tensor(f"in_{short}", a.shape, mybir.dt.from_np(a.dtype), kind="ExternalInput").ap()
    arrays["in_eye"] = np.eye(P, dtype=np.float32)
    io["eye"] = nc.dram_tensor("in_eye", (P, P), F32, kind="ExternalInput").ap()
    B, N, D, H, E = dims(io["x"], io["adj"], io["W"])
    io["hu"] = nc.dram_tensor("scratch_hu", (B * N, D + 4 * H), F32, kind="Internal").ap()
    io["out"] = nc.dram_tensor("out", (B, N, D), F32, kind="ExternalOutput").ap()
    gat_layer(nc, io)
    r = run_bass_kernel_spmd(nc, [arrays], core_ids=[0])
    return r.results[0]["out"]
```

```python
import math
from contextlib import ExitStack

import concourse.bass as bass
from concourse import mybir

P = 128
F16 = mybir.dt.float16
BF16 = mybir.dt.bfloat16
F32 = mybir.dt.float32
I32 = mybir.dt.int32
ALU = mybir.AluOpType
ACT = mybir.ActivationFunctionType
AX = mybir.AxisListType
RMAX = bass.bass_isa.ReduceOp.max

LEAK = 0.01
EPS_HEAD = 1e-6
EPS_ROW = 1e-5

V_SCALE = 4.0
LN_V_SCALE = math.log(V_SCALE)
EXP_SQ = 39.0
H_SQ = 700.0
BIAS_SQ = 9.0
DEN_LEAST = 1e-6

TPB = 4
A16_SLOTS = 4
RAMPS = (7, 5, 8, 7)
EARLY_RAMPS = 3
STEEP = 2.0 ** 40
NA_SLOTS = 4
FIRST = 1


def dims(x, adj, W):
    B, N, D = x.shape
    H, E = W.shape[0], W.shape[2]
    return B, N, D, H, E


def main_path(nc, io, viol_i, sems):
    x, adj, W = io["x"], io["adj"], io["W"]
    B, N, D, H, E = dims(x, adj, W)
    JT = N // P
    NT = B * JT
    BLK = TPB * P
    NB = NT // TPB
    KD = D // P
    E1 = E + 1
    HC = D + 4 * H
    CH = N // 2
    CPB = 2 * TPB
    BPB = JT // TPB
    HALF = JT // 2
    HP_NA = D + 2 * H
    RW = 3 * E1
    assert H == TPB == 4 and D == 2 * P and JT == 16 and E == 64

    x_t = x.rearrange("b (t p) d -> p (b t) d", p=P)
    out_t = io["out"].rearrange("b (t p) d -> p (b t) d", p=P)
    adj_t = adj.rearrange("b (t p) n -> p (b t) n", p=P)
    hu_t = io["hu"].rearrange("(t p) c -> p t c", p=P)

    with ExitStack() as ctx:
        def sb(name, shape, dt=F32):
            return ctx.enter_context(nc.sbuf_tensor(name, shape, dt))

        def psum(name, shape, dt=F32):
            return ctx.enter_context(nc.psum_tensor(name, shape, dt))

        def sem(name):
            return sems.enter_context(nc.semaphore(name))

        ident = sb("ident", [P, P])
        sel = sb("sel", [TPB * H, TPB * H, P], F16)
        wa = sb("wa", [P, KD, D + 2 * H])
        bias_bc = sb("bias_bc", [P, D])
        gamma_bc = sb("gamma_bc", [P, D])
        beta_bc = sb("beta_bc", [P, D])
        neg_half = sb("neg_half", [P, 1])
        ln_scale = sb("ln_scale", [P, 1])
        exponent = sb("exponent", [P, TPB * H])
        xin = sb("xin", [P, 2, D])
        xT = sb("xT", [P, KD, P])
        hb = sb("hb", [P, H, E1])
        vh32 = sb("vh32", [P, 2, H, E1])
        vh = sb("vh", [P, 2 * JT, H, 2, 2, E1], F16)
        bcol = sb("bcol", [P, 2 * JT, H])
        bcol_steep = sb("bcol_steep", [P, 2 * JT, H])
        ramp = sb("ramp", [P, max(RAMPS), BLK], BF16)
        na_c = sb("na_c", [P, H, TPB])
        na_t = sb("na_t", [TPB * H, NA_SLOTS, 2, P], F16)
        hu_out = sb("hu_out", [P, TPB, HC])
        hu_in = sb("hu_in", [P, 2, TPB, HC])
        a16 = sb("a16", [P, A16_SLOTS, CH], F16)
        mt = sb("mt", [P, 2, JT, BLK], F16)
        g_sb = sb("g_sb", [P, 2, JT, BLK], F16)
        dens = sb("dens", [P, 2, 2, 3])
        den_e = sb("den_e", [P, 2, 2])
        den_m = sb("den_m", [P, 2, 2, 2])
        den = sb("den", [P, TPB])
        rden_in = sb("rden_in", [P, TPB])
        rden = sb("rden", [P, TPB])
        cw = sb("cw", [P, 2, TPB])
        m_sum = sb("m_sum", [P, 2, 2, E])
        t1 = sb("t1", [P, TPB, E])
        e2 = sb("e2", [P, TPB, E])
        att = sb("att", [P, 2, TPB, D])
        x_res = sb("x_res", [P, 2, TPB, D])
        sq = sb("sq", [P, TPB, D])
        s_head = sb("s_head", [P, 2, TPB * H])
        m_head = sb("m_head", [P, TPB * H])
        r_head = sb("r_head", [P, TPB * H])
        s_row = sb("s_row", [P, 2, TPB])
        m_row = sb("m_row", [P, TPB])
        r_row = sb("r_row", [P, TPB])
        n_row = sb("n_row", [P, TPB])
        scrap = sb("scrap", [P, CH], BF16)
        scrap_e = sb("scrap_e", [P, 2 * H])
        scrap_h = sb("scrap_h", [P, D], BF16)
        slopes = sb("slopes", [P, 2])
        in_exp = sb("in_exp", [P, 2])
        in_range = sb("in_range", [P, 2])
        met_adj = sb("met_adj", [P, NB * CPB])
        met_exp = sb("met_exp", [P, NT + 1])
        met_h = sb("met_h", [P, NT + 1])
        met_den = sb("met_den", [P, TPB])
        worst = sb("worst", [P, 5])
        broken = sb("broken", [P, 6])
        broken_all = sb("broken_all", [P, 1])

        acc = psum("acc", [P, 4, 512])
        na = psum("na", [P, 2, 512])
        turn = psum("turn", [P, 512])
        hp = psum("hp", [P, 512])

        consts_in = sem("consts_in")
        gamma_in = sem("gamma_in")
        consts_set = sem("consts_set")
        wa_done = sem("wa_done")
        x_in = [sem(f"x_in{i}") for i in range(2)]
        x_turned = sem("x_turned")
        xT_copied = sem("xT_copied")
        h_made = sem("h_made")
        exps_made = sem("exps_made")
        h_read_act = sem("h_read_act")
        h_read_dve = sem("h_read_dve")
        na_turned = sem("na_turned")
        na_hi_done = sem("na_hi_done")
        na_split = sem("na_split")
        na_made = sem("na_made")
        hu_stored = [sem(f"hu_stored{i}") for i in range(2)]
        hb_made = sem("hb_made")
        vh32_made = sem("vh32_made")
        vh_hi_done = sem("vh_hi_done")
        vh_done = sem("vh_done")
        a16_in = [sem(f"a16_in{i}") for i in range(A16_SLOTS)]
        adj_checked = sem("adj_checked")
        turned = [sem(f"turned{i}") for i in range(A16_SLOTS)]
        ramp_made = sem("ramp_made")
        g_made = sem("g_made")
        unit_done = sem("unit_done")
        dens_read = sem("dens_read")
        m_read = sem("m_read")
        den_step = sem("den_step")
        den_made = sem("den_made")
        rden_safe = sem("rden_safe")
        rden_made = sem("rden_made")
        cw_made = sem("cw_made")
        t1_made = sem("t1_made")
        e2_made = sem("e2_made")
        att_made = sem("att_made")
        res_in = sem("res_in")
        o_made = sem("o_made")
        s1_made = sem("s1_made")
        mean_made = sem("mean_made")
        cent_made = sem("cent_made")
        sq_made = sem("sq_made")
        s2_made = sem("s2_made")
        norm_step = sem("norm_step")
        xb_made = sem("xb_made")
        in_range_step = sem("in_range_step")
        z_made = sem("z_made")
        s3_made = sem("s3_made")
        m2_made = sem("m2_made")
        s4_made = sem("s4_made")
        r2_made = sem("r2_made")
        fin_made = sem("fin_made")
        out_stored = sem("out_stored")
        met_done = sem("met_done")
        viol_step = sem("viol_step")
        viol_step_dve = sem("viol_step_dve")
        stood = {e.engine: sem(f"stood_{n}") for n, e in
                 (("sp", nc.sync), ("pool", nc.gpsimd), ("act", nc.scalar), ("dve", nc.vector), ("pe", nc.tensor))}

        block = ctx.enter_context(nc.Block())

        def region(u_slot, it):
            c = (it % 2) * RW
            return acc[:, 2 * u_slot + it // 2, c:c + RW]

        def regions(u_slot, c0, c1):
            r = acc[:, 2 * u_slot:2 * u_slot + 2, 0:2 * RW]
            return r.rearrange("p k (i c) -> p k i c", c=RW)[:, :, :, c0:c1]

        def batch_slot(t):
            return t % (2 * JT)

        def tail_of(ap, n):
            k = len(ap.shape)
            return ap.unsqueeze(k).to_broadcast([*ap.shape, n])

        def stand(eng):
            eng.sem_inc(stood[eng.engine], 1)

        from_first = (z_made, unit_done, out_stored, mean_made, norm_step, na_split, att_made, exps_made,
                      *hu_stored)

        hp_before = (hp, acc[:, 3, :])

        na_turn = hp[0:TPB * H, HP_NA:HP_NA + P]


        @block.sync
        def _(sp):
            def load_x(t, slot, turned_before):
                sp.wait_ge(x_turned, turned_before)
                stand(sp)
                sp.dma_start(xin[:, slot, :].unsqueeze(1), x_t[:, bass.ds(t, 1), :]).then_inc(x_in[slot], 16)

            def transpose_chunk(g, k, mt_slot):
                slot = k % A16_SLOTS
                it, half = k // 2, k % 2
                sp.wait_ge(a16_in[slot], (g * (CPB // A16_SLOTS) + k // A16_SLOTS + 1) * 16)
                stand(sp)
                dst = mt[:, mt_slot, half * HALF:(half + 1) * HALF, it * P:(it + 1) * P]
                sp.dma_start_transpose(dst, a16[:, slot, :]).then_inc(turned[slot], 16)

            def load_residual(g):
                sp.wait_ge(res_in, g * 32)
                stand(sp)
                for part in hu_stored:
                    sp.wait_ge(part, FIRST + g * 16 + 16)
                    stand(sp)
                dst = hu_in[:, bass.ds(g % 2, 1), :, :].rearrange("p a t c -> p (a t) c")
                sp.dma_start(dst, hu_t[:, bass.ds(g * TPB, TPB), :]).then_inc(res_in, 16)
                dst = x_res[:, bass.ds(g % 2, 1), :, :].rearrange("p a t c -> p (a t) c")
                sp.dma_start(dst, x_t[:, bass.ds(g * TPB, TPB), :]).then_inc(res_in, 16)

            for first in from_first:
                sp.sem_inc(first, FIRST)
            for k in range(KD):
                dst = wa[:, k, 0:D].rearrange("p (h e) -> p h e", h=H)
                src = W.rearrange("h (k p) e -> k p h e", p=P)[k]
                sp.dma_start(dst, src).then_inc(consts_in, 16)
            for i, src in enumerate((io["a_src"], io["a_dst"])):
                dst = sq[:, i, :].rearrange("p (h e) -> p h e", h=H)
                sp.dma_start(dst, src[:, 0, :].partition_broadcast(P)).then_inc(consts_in, 16)
            sp.dma_start(ident[:], io["eye"]).then_inc(consts_in, 16)
            sp.dma_start(bias_bc[:].rearrange("p (h e) -> p h e", h=H), io["bias"].partition_broadcast(P))\
                .then_inc(consts_in, 16)

            def prep(p, t):
                T = p * TPB + t
                load_x((T + 1) % NT, (t + 1) % 2, T)

            load_x(0, 0, 0)
            load_x(1, 1, 0)
            for tile, src in ((gamma_bc, io["gamma"]), (beta_bc, io["beta"])):
                dst = tile[:].rearrange("p (h e) -> p h e", h=H)
                sp.dma_start(dst, src.partition_broadcast(P)).then_inc(gamma_in, 16)
            for k in range(CPB):
                transpose_chunk(0, k, 0)
            with sp.Fori(0, BPB) as p:
                for t in range(1, TPB + 1):
                    prep(p, t)

            def step(g, more=False, last=False):
                for h in range(H):
                    if more:
                        prep(g + BPB, h + 1)
                    if h == 0 and not last:
                        sp.wait_ge(unit_done, FIRST + g * H)
                    stand(sp)
                    if not last:
                        for k in ((0, 1, 2), (3, 4, 5), (6, 7), ())[h]:
                            slot = k % A16_SLOTS
                            it, half = k // 2, k % 2
                            sp.wait_ge(a16_in[slot], (g * 2 + 2 + k // A16_SLOTS + 1) * 16)
                            stand(sp)
                            dst = mt[:, bass.ds((g + 1) % 2, 1), half * HALF:(half + 1) * HALF, it * P:(it + 1) * P]
                            sp.dma_start_transpose(dst.rearrange("p a j i -> p (a j) i"),
                                                   a16[:, slot, :]).then_inc(turned[slot], 16)
                    if h == 0:
                        if not (isinstance(g, int) and g == 0):
                            sp.wait_ge(z_made, FIRST + g - 1)
                        stand(sp)
                        load_residual(g)

            step(0, more=True)
            with sp.Fori(1, NB - BPB) as g:
                step(g, more=True)
            with sp.Fori(NB - BPB, NB - 1) as g:
                step(g)
            step(NB - 1, last=True)

        @block.gpsimd
        def _(pool):
            def load_chunk(g, k, ahead):
                slot = k % A16_SLOTS
                if ahead:
                    pool.wait_ge(turned[slot], (g * 2 + k // A16_SLOTS) * 16)
                    pool.wait_ge(adj_checked, g * CPB + k - A16_SLOTS + 1)
                stand(pool)
                src = adj_t[:, bass.ds(g * TPB + k // 2, 1), (k % 2) * CH:(k % 2) * CH + CH]
                pool.dma_start(a16[:, slot, :].unsqueeze(1), src).then_inc(a16_in[slot], 16)

            def weigh(t, slot):
                pool.wait_ge(hb_made, t + 1)
                pool.wait_ge(exps_made, FIRST + t + 1)
                pool.wait_ge(vh_done, t)
                stand(pool)
                w = hu_out[:, slot, D:HC].rearrange("p (f s h) -> p f s h", f=2, s=2)[:, :, 1, :]
                for f in range(2):
                    pool.tensor_tensor(vh32[:, f, :, :], hb[:, :, :], tail_of(w[:, f, :], E1), ALU.mult)\
                        .then_inc(vh32_made, 1)

            def low_parts(t):
                pool.wait_ge(vh_hi_done, t * 2 + 2)
                stand(pool)
                for f in range(2):
                    v = vh[:, bass.ds(batch_slot(t), 1), :, :, f, :].rearrange("p a h s e -> p (a h) s e")
                    ins = pool.tensor_tensor(v[:, :, 1, :], vh32[:, f, :, :], v[:, :, 0, :], ALU.subtract)
                ins.then_inc(vh_done, 1)

            def exps_of(g, h):
                e = hu_in[:, bass.ds(g % 2, 1), :, D:HC].rearrange("p a t c -> p (a t) c")
                return e.rearrange("p t (f s h) -> p f s h t", f=2, s=2)[:, :, 0, h, :]

            def denominator(g, h, u):
                pool.wait_ge(dens_read, u + 1)
                if h == 0:
                    pool.wait_ge(res_in, g * 32 + 32)
                stand(pool)
                ks = "p (k i) -> p k i"
                e = exps_of(g, h)
                pool.tensor_tensor(den_e[:], dens[:, :, :, 2], dens[:, :, :, 1], ALU.subtract).then_inc(den_step, 1)
                pool.tensor_tensor(den_m[:, 0, :, :], dens[:, :, :, 0], e[:, 0, :].rearrange(ks, k=2), ALU.mult)\
                    .then_inc(den_step, 1)
                pool.wait_ge(den_step, u * 3 + 2)
                stand(pool)
                pool.tensor_tensor(den_m[:, 1, :, :], den_e[:], e[:, 1, :].rearrange(ks, k=2), ALU.mult)\
                    .then_inc(den_step, 1)
                pool.wait_ge(den_step, u * 3 + 3)
                pool.wait_ge(rden_made, u)
                stand(pool)
                pool.tensor_tensor(den[:].rearrange(ks, k=2), den_m[:, 0, :, :], den_m[:, 1, :, :], ALU.add)\
                    .then_inc(den_made, 1)

            def weights(g, h, u):
                pool.wait_ge(rden_made, u + 1)
                pool.wait_ge(att_made, FIRST + u)
                stand(pool)
                e = exps_of(g, h)
                pool.tensor_tensor(cw[:], e, rden[:].unsqueeze(1).to_broadcast([P, 2, TPB]), ALU.mult)\
                    .then_inc(cw_made, 1)

            def head_mean(g):
                pool.wait_ge(s1_made, g + 1)
                stand(pool)
                pool.tensor_scalar(m_head[:], s_head[:, 0, :], -1.0 / E, 0.0, ALU.mult, ALU.add).then_inc(mean_made, 1)

            def centre(g):
                pool.wait_ge(mean_made, FIRST + g + 1)
                stand(pool)
                a = att[:, bass.ds(g % 2, 1), :, :].rearrange("p a t d -> p (a t) d")
                ah = a.rearrange("p t (h e) -> p (t h) e", h=H)
                pool.tensor_tensor(ah, ah, tail_of(m_head[:], E), ALU.add).then_inc(cent_made, 1)

            def head_scale(g):
                pool.wait_ge(s2_made, g + 1)
                stand(pool)
                n = g * 4
                pool.tensor_scalar(s_head[:, 1, :], s_head[:, 1, :], 1.0 / E, EPS_HEAD, ALU.mult, ALU.add)\
                    .then_inc(norm_step, 1)
                pool.wait_ge(norm_step, FIRST + n + 1)
                stand(pool)
                pool.tensor_tensor(r_head[:], s_head[:, 1, :], exponent[:], ALU.pow).then_inc(norm_step, 1)
                pool.wait_ge(norm_step, FIRST + n + 2)
                stand(pool)
                a = att[:, bass.ds(g % 2, 1), :, :].rearrange("p a t d -> p (a t) d")
                ah = a.rearrange("p t (h e) -> p (t h) e", h=H)
                pool.tensor_tensor(ah, ah, tail_of(r_head[:], E), ALU.mult).then_inc(norm_step, 1)

            def head_gamma(g):
                a = att[:, bass.ds(g % 2, 1), :, :].rearrange("p a t d -> p (a t) d")
                pool.wait_ge(norm_step, FIRST + g * 4 + 3)
                stand(pool)
                pool.tensor_tensor(a, a, gamma_bc[:].unsqueeze(1).to_broadcast([P, TPB, D]), ALU.mult)\
                    .then_inc(norm_step, 1)

            def x_of(g):
                return x_res[:, bass.ds(g % 2, 1), :, :].rearrange("p a t d -> p (a t) d")

            def add_beta(g):
                pool.wait_ge(res_in, g * 32 + 32)
                stand(pool)
                pool.tensor_tensor(x_of(g), x_of(g), beta_bc[:].unsqueeze(1).to_broadcast([P, TPB, D]), ALU.add)\
                    .then_inc(xb_made, 1)

            def add_x(g):
                a = att[:, bass.ds(g % 2, 1), :, :].rearrange("p a t d -> p (a t) d")
                pool.wait_ge(norm_step, FIRST + g * 4 + 4)
                pool.wait_ge(xb_made, g + 1)
                stand(pool)
                pool.tensor_tensor(a, a, x_of(g), ALU.add).then_inc(z_made, 1)

            def row_mean(g):
                pool.wait_ge(s3_made, g * TPB + TPB)
                stand(pool)
                pool.tensor_scalar(m_row[:], s_row[:, 0, :], -1.0 / D, 0.0, ALU.mult, ALU.add).then_inc(m2_made, 1)

            def row_scale(g):
                pool.wait_ge(s4_made, g * TPB + TPB)
                stand(pool)
                n = g * 3
                pool.tensor_scalar(s_row[:, 1, :], s_row[:, 1, :], 1.0 / D, EPS_ROW, ALU.mult, ALU.add)\
                    .then_inc(r2_made, 1)
                pool.wait_ge(r2_made, n + 1)
                stand(pool)
                pool.tensor_tensor(r_row[:], s_row[:, 1, :], exponent[:, 0:TPB], ALU.pow).then_inc(r2_made, 1)
                pool.wait_ge(r2_made, n + 2)
                stand(pool)
                pool.tensor_tensor(n_row[:], m_row[:], r_row[:], ALU.mult).then_inc(r2_made, 1)

            for k in range(A16_SLOTS):
                load_chunk(0, k, False)
            pool.wait_ge(consts_set, 9)
            pool.wait_ge(gamma_in, 32)
            stand(pool)
            for k in range(A16_SLOTS, CPB + A16_SLOTS):
                load_chunk(0, k, True)
            weigh(0, 0)
            with pool.Fori(0, BPB) as p:
                for t in range(1, TPB + 1):
                    low_parts(p * TPB + t - 1)
                    weigh(p * TPB + t, t % TPB)

            def step(g, more=False, first=False, last=False):
                for h in range(H):
                    u = g * H + h
                    before = (g, h - 1) if h else (g - 1, H - 1)
                    if not (first and h == 0):
                        denominator(*before, u - 1)
                        weights(*before, u - 1)
                    if more:
                        low_parts(u + JT)
                    if not first and h == 3:
                        head_gamma(g - 1)
                        add_x(g - 1)
                    if not first:
                        if h == 1:
                            head_mean(g - 1)
                            centre(g - 1)
                            add_beta(g - 1)
                        if h == 2:
                            head_scale(g - 1)
                        if h == 3:
                            row_mean(g - 1)
                    for k in ((0, 1, 2), (3, 4, 5), (6, 7), ())[h]:
                        if not last and not (isinstance(g, int) and g == NB - 2 and k >= A16_SLOTS):
                            load_chunk(g + 1, A16_SLOTS + k, True)
                    if more:
                        weigh(u + JT + 1, (h + 1) % TPB)
                    if not first:
                        if h == 3:
                            row_scale(g - 1)

            step(0, more=True, first=True)
            with pool.Fori(1, NB - BPB) as g:
                step(g, more=True)
            with pool.Fori(NB - BPB, NB - 2) as g:
                step(g)
            step(NB - 2)
            step(NB - 1, last=True)
            denominator(NB - 1, H - 1, NB * H - 1)
            weights(NB - 1, H - 1, NB * H - 1)
            add_beta(NB - 1)
            head_mean(NB - 1)
            centre(NB - 1)
            head_scale(NB - 1)
            head_gamma(NB - 1)
            add_x(NB - 1)
            row_mean(NB - 1)
            row_scale(NB - 1)
            pool.wait_ge(met_done, 1)
            stand(pool)
            pool.partition_all_reduce(broken_all[:], broken[:, 5:6], P, RMAX).then_inc(viol_step, 1)
            pool.wait_ge(viol_step, 1)
            stand(pool)
            pool.tensor_copy(viol_i[:, :], broken_all[:]).then_inc(viol_step, 1)
            pool.wait_ge(viol_step, 2)
            stand(pool)

        @block.scalar
        def _(act):
            def copy_xT(t):
                act.wait_ge(x_turned, t + 1)
                act.wait_ge(h_made, t)
                stand(act)
                act.activation(xT[:, :, :], turn[:, 0:D].rearrange("p (k i) -> p k i", k=KD), ACT.Copy)\
                    .then_inc(xT_copied, 1)

            def read_h(t, slot, stored=None, hp=hp):
                act.wait_ge(h_made, t + 1)
                if stored is not None:
                    act.wait_ge(*stored)
                stand(act)
                act.activation(bcol_steep[:, bass.ds(batch_slot(t), 1), :].rearrange("p a h -> p (a h)"),
                               hp[:, D + H:D + 2 * H], ACT.Copy, scale=STEEP)
                act.activation(scrap_e[:], hp[:, D:D + 2 * H], ACT.Square,
                               accum_out=met_exp[:, bass.ds(t, 1)])
                act.activation(scrap_h[:], hp[:, 0:D], ACT.Square,
                               accum_out=met_h[:, bass.ds(t, 1)])
                act.activation(hu_out[:, slot, 0:D], hp[:, 0:D], ACT.Copy).then_inc(h_read_act, 1)

            def exponentials(t, slot, hp=hp):
                act.wait_ge(h_read_dve, t + 1)
                stand(act)
                act.activation(hu_out[:, slot, D:D + 2 * H], hp[:, D:D + 2 * H], ACT.Exp,
                               bias=ln_scale[:, 0:1], scale=in_range[:, 0:1])
                act.activation(hu_out[:, slot, D + 2 * H:HC], hp[:, D:D + 2 * H], ACT.Exp,
                               bias=ln_scale[:, 0:1], scale=in_range[:, 1:2]).then_inc(exps_made, 1)

            def slot_stored(p, t):
                if t == TPB:
                    return hu_stored[0], FIRST + (p + 1) * 16
                if t == TPB - 1:
                    return hu_stored[1], FIRST + p * 16
                return None

            def store_hu(p, part):
                t0, t1 = ((0, TPB - 1), (TPB - 1, TPB))[part]
                act.wait_ge(h_read_act, p * TPB + t1)
                act.wait_ge(exps_made, FIRST + p * TPB + t1)
                stand(act)
                act.dma_start(hu_t[:, bass.ds(p * TPB + t0, t1 - t0), :], hu_out[:, t0:t1, :])\
                    .then_inc(hu_stored[part], 16)

            def high_parts(t):
                act.wait_ge(vh32_made, t * 2 + 2)
                stand(act)
                for f in range(2):
                    dst = vh[:, bass.ds(batch_slot(t), 1), :, 0, f, :].rearrange("p a h e -> p (a h) e")
                    act.activation(dst, vh32[:, f, :, :], ACT.Copy).then_inc(vh_hi_done, 1)

            def na_high(p):
                act.wait_ge(na_turned, p + 1)
                act.wait_ge(h_made, (p + 1) * TPB + 1)
                stand(act)
                dst = na_t[:, bass.ds(p % NA_SLOTS, 1), 0, :].rearrange("p a i -> p (a i)")
                act.activation(dst, na_turn, ACT.Copy).then_inc(na_hi_done, 1)

            def ramps(g, h, u, jt0, jt1):
                act.wait_ge(na_made, u + 1)
                stand(act)
                for jt in range(jt0, jt1):
                    if not (isinstance(u, int) and u == 0):
                        act.wait_ge(g_made, (u - 1) * JT + jt + 1)
                    stand(act)
                    b = bcol_steep[:, bass.ds((g // BPB % 2) * JT + jt, 1), h]
                    act.activation(ramp[:, jt, :], na[:, h % 2, :], ACT.Relu, bias=b, scale=-STEEP)\
                        .then_inc(ramp_made, 1)

            def check_chunk(g, k):
                slot = k % A16_SLOTS
                act.wait_ge(a16_in[slot], (g * 2 + k // A16_SLOTS + 1) * 16)
                if not (isinstance(g, int) and g == 0 and k == 0):
                    act.wait_ge(adj_checked, g * CPB + k)
                stand(act)
                act.activation(scrap[:], a16[:, slot, :], ACT.Square, bias=neg_half[:, 0:1],
                               accum_out=met_adj[:, bass.ds(g * CPB + k, 1)]).then_inc(adj_checked, 1)

            def read_sums(s, u):
                act.wait_ge(unit_done, FIRST + u + 1)
                act.wait_ge(den_made, u)
                stand(act)
                act.activation(dens[:], regions(s, E, RW)[:, :, :, ::E1], ACT.Copy).then_inc(dens_read, 1)
                act.wait_ge(e2_made, u)
                stand(act)
                act.activation(m_sum[:], regions(s, 2 * E1, 2 * E1 + E), ACT.Copy).then_inc(m_read, 1)

            def first_terms(s, u):
                act.wait_ge(cw_made, u + 1)
                act.wait_ge(att_made, FIRST + u)
                stand(act)
                for it in range(TPB):
                    act.activation(t1[:, it, :], region(s, it)[:, 0:E], ACT.Copy, scale=cw[:, 0, it:it + 1])\
                        .then_inc(t1_made, 1)

            def att_of(g):
                return att[:, bass.ds(g % 2, 1), :, :].rearrange("p a t d -> p (a t) d")

            def squares(g):
                act.wait_ge(cent_made, g + 1)
                stand(act)
                act.activation(sq[:], att_of(g), ACT.Square).then_inc(sq_made, 1)

            def row_sums(g):
                act.wait_ge(z_made, FIRST + g + 1)
                stand(act)
                for it in range(TPB):
                    act.activation(sq[:, it, :], att_of(g)[:, it, :], ACT.Copy, accum_out=s_row[:, 0, it:it + 1])\
                        .then_inc(s3_made, 1)

            def row_squares(g):
                act.wait_ge(m2_made, g + 1)
                stand(act)
                for it in range(TPB):
                    act.activation(sq[:, it, :], att_of(g)[:, it, :], ACT.Square, bias=m_row[:, it:it + 1],
                                   accum_out=s_row[:, 1, it:it + 1]).then_inc(s4_made, 1)

            def finish_rows(g):
                act.wait_ge(r2_made, g * 3 + 3)
                act.wait_ge(out_stored, FIRST + g * 16)
                stand(act)
                for it in range(TPB):
                    act.activation(att_of(g)[:, it, :], att_of(g)[:, it, :], ACT.Identity, bias=n_row[:, it:it + 1],
                                   scale=r_row[:, it:it + 1]).then_inc(fin_made, 1)
                act.wait_ge(fin_made, g * TPB + TPB)
                stand(act)
                act.dma_start(out_t[:, bass.ds(g * TPB, TPB), :], att_of(g)).then_inc(out_stored, 16)

            act.wait_ge(consts_set, 9)
            stand(act)
            copy_xT(0)
            read_h(0, 0)
            exponentials(0, 0)
            copy_xT(1)
            for k in range(CPB + 3):
                check_chunk(0, k)
            def prep(p):
                for t in range(1, TPB + 1):
                    T = p * TPB + t
                    if t == TPB:
                        na_high(p)
                    read_h(T, t % TPB, slot_stored(p, t), hp_before[t % 2])
                    copy_xT(T + 1)
                    high_parts(T - 1)
                    exponentials(T, t % TPB, hp_before[t % 2])
                    if t in (TPB - 2, TPB - 1):
                        store_hu(p, t - (TPB - 2))

            with act.Fori(0, BPB - 1) as p:
                prep(p)
            ramps(0, 0, 0, 0, RAMPS[0])
            prep(BPB - 1)
            ramps(0, 1, 1, 0, RAMPS[1])

            def step(g, more=False, first=False, second=False, last=False):
                for h in range(H):
                    u = g * H + h
                    T = u + JT + 1
                    s_before = (h + 1) % 2
                    if not (first and h == 0):
                        read_sums(s_before, u - 1)
                    if more:
                        if h == 0:
                            act.wait_ge(unit_done, FIRST + (g // BPB) * (H * BPB))
                        stand(act)
                        high_parts(T - 1)
                    checks = ((3,), (4, 5, 6), (7, 8, 9), (10,))[h]
                    if last or isinstance(g, int) and g == NB - 2:
                        checks = [] if last else [k for k in checks if k < CPB]
                    for k in checks[:1]:
                        check_chunk(g + 1, k)
                    after = (g + (h + 2) // H, (h + 2) % H, u + 2)
                    if not (last and h >= 2):
                        ramps(*after, 0, EARLY_RAMPS)
                    if more and h == H - 1:
                        na_high(g + BPB)
                    if more:
                        read_h(T, (h + 1) % TPB, slot_stored(g + BPB, h + 1))
                    if not (first and h == 0):
                        first_terms(s_before, u - 1)
                    if not (last and h >= 2):
                        ramps(*after, EARLY_RAMPS, RAMPS[after[1]])
                    if not first and h == 3:
                        row_sums(g - 1)
                    for k in checks[1:]:
                        check_chunk(g + 1, k)
                    if more:
                        exponentials(T, (h + 1) % TPB)
                        if h in (1, 2):
                            store_hu(g + BPB, h - 1)
                        copy_xT(T + 1)
                    if not first:
                        if h == 1:
                            squares(g - 1)
                        if h == 3:
                            row_squares(g - 1)
                        if h == 0 and not second:
                            finish_rows(g - 2)

            step(0, more=True, first=True)
            step(1, more=True, second=True)
            with act.Fori(2, NB - BPB) as g:
                step(g, more=True)
            with act.Fori(NB - BPB, NB - 2) as g:
                step(g)
            step(NB - 2)
            step(NB - 1, last=True)
            read_sums((NB * H - 1) % 2, NB * H - 1)
            first_terms((NB * H - 1) % 2, NB * H - 1)
            finish_rows(NB - 2)
            squares(NB - 1)
            row_sums(NB - 1)
            row_squares(NB - 1)
            finish_rows(NB - 1)
            act.wait_ge(out_stored, FIRST + NB * 16)
            stand(act)

        @block.vector
        def _(dve):
            def make_g(g, h, u, jt):
                b = bcol[:, bass.ds((g // BPB % 2) * JT + jt, 1), h]
                m = mt[:, bass.ds(g % 2, 1), jt, :].rearrange("p a i -> p (a i)")
                if jt < RAMPS[h]:
                    dve.tensor_tensor(g_sb[:, h % 2, jt, :], ramp[:, jt, :], m, ALU.min).then_inc(g_made, 1)
                    return
                dve.scalar_tensor_tensor(out=g_sb[:, h % 2, jt, :], in0=na[:, h % 2, :], scalar=b, in1=m,
                                         op0=ALU.is_lt, op1=ALU.mult).then_inc(g_made, 1)

            def before_g(g, h, u):
                dve.wait_ge(na_made, u + 1)
                dve.wait_ge(ramp_made, g * sum(RAMPS) + sum(RAMPS[:h + 1]))
                if not (isinstance(u, int) and u < 2):
                    dve.wait_ge(unit_done, FIRST + u - 1)
                if h == 0:
                    dve.wait_ge(h_read_dve, (g // BPB + 1) * JT)
                    for slot in range(A16_SLOTS):
                        dve.wait_ge(turned[slot], (g + 1) * (CPB // A16_SLOTS) * 16)

            def before_first_g():
                dve.wait_ge(na_made, 1)
                dve.wait_ge(ramp_made, RAMPS[0])
                dve.wait_ge(h_read_dve, 3 * TPB)
                for slot in range(A16_SLOTS):
                    dve.wait_ge(turned[slot], (CPB // A16_SLOTS) * 16)

            def na_low(p):
                dve.wait_ge(na_hi_done, p + 1)
                n = na_t[:, bass.ds(p % NA_SLOTS, 1), :, :].rearrange("p a s i -> p (a s) i")
                dve.tensor_tensor(n[:, 1, :], na_turn, n[:, 0, :], ALU.subtract).then_inc(na_split, 1)

            def add_bias(t, slot, hp=hp, p=None):
                dve.wait_ge(h_read_act, t + 1)
                if p is not None:
                    na_low(p)
                dve.wait_ge(vh32_made, t * 2)
                dve.scalar_tensor_tensor(out=in_exp[:], in0=met_exp[:, bass.ds(t, 1)].to_broadcast([P, 2]),
                                         scalar=EXP_SQ, in1=slopes[:], op0=ALU.is_le, op1=ALU.mult)\
                    .then_inc(in_range_step, 1)
                dve.tensor_scalar(na_c[:, :, slot], hp[:, D:D + H], -1.0, None, ALU.mult)
                dst = bcol[:, bass.ds(batch_slot(t), 1), :].rearrange("p a h -> p (a h)")
                dve.tensor_copy(dst, hp[:, D + H:D + 2 * H])
                dst = hb[:, :, 0:E]
                src = hp[:, 0:D].rearrange("p (h e) -> p h e", h=H)
                dve.tensor_tensor(dst, src, bias_bc[:].rearrange("p (h e) -> p h e", h=H), ALU.add).then_inc(hb_made, 1)
                dve.wait_ge(in_range_step, t + 1)
                dve.scalar_tensor_tensor(out=in_range[:], in0=met_h[:, bass.ds(t, 1)].to_broadcast([P, 2]),
                                         scalar=H_SQ, in1=in_exp[:], op0=ALU.is_le, op1=ALU.mult)\
                    .then_inc(h_read_dve, 1)

            def reciprocals(u):
                dve.wait_ge(den_made, u + 1)
                dve.wait_ge(cw_made, u)
                dve.tensor_tensor(met_den[:], met_den[:], den[:], ALU.min).then_inc(rden_safe, 1)
                dve.tensor_scalar(rden_in[:], den[:], DEN_LEAST, None, ALU.max).then_inc(rden_safe, 1)
                dve.wait_ge(rden_safe, u * 2 + 2)
                dve.reciprocal(rden[:], rden_in[:]).then_inc(rden_made, 1)

            def second_terms(g, h, u, s):
                dve.wait_ge(m_read, u + 1)
                dve.wait_ge(t1_made, u * TPB + TPB)
                e = e2[:].rearrange("p (k i) e -> p k i e", k=2)
                dve.tensor_tensor(e, m_sum[:], regions(s, E1, E1 + E), ALU.subtract).then_inc(e2_made, 1)
                dve.wait_ge(e2_made, u + 1)
                if h == 0 and not (isinstance(g, int) and g < 2):
                    dve.wait_ge(out_stored, FIRST + (g - 1) * 16)
                for it in range(TPB):
                    dst = att[:, bass.ds(g % 2, 1), it, h * E:(h + 1) * E].rearrange("p a e -> p (a e)")
                    ins = dve.scalar_tensor_tensor(out=dst, in0=e2[:, it, :], scalar=cw[:, 1, it:it + 1],
                                                   in1=t1[:, it, :], op0=ALU.mult, op1=ALU.add)
                ins.then_inc(att_made, 1)

            def att_of(g):
                return att[:, bass.ds(g % 2, 1), :, :].rearrange("p a t d -> p (a t) d")

            def residual(g):
                dve.wait_ge(att_made, FIRST + g * H + H)
                dve.wait_ge(res_in, g * 32 + 32)
                hh = hu_in[:, bass.ds(g % 2, 1), :, 0:D].rearrange("p a t d -> p (a t) d")
                dve.scalar_tensor_tensor(out=att_of(g), in0=att_of(g), scalar=0.0, in1=hh,
                                         op0=ALU.max, op1=ALU.add).then_inc(o_made, 1)
                dve.wait_ge(mean_made, FIRST + g)
                dve.wait_ge(o_made, g + 1)
                stand(dve)
                dve.reduce_sum(s_head[:, 0, :], att_of(g).rearrange("p t (h e) -> p (t h) e", h=H), AX.X)\
                    .then_inc(s1_made, 1)

            def square_sums(g):
                dve.wait_ge(sq_made, g + 1)
                dve.wait_ge(norm_step, FIRST + g * 4)
                stand(dve)
                dve.reduce_sum(s_head[:, 1, :], sq[:].rearrange("p t (h e) -> p (t h) e", h=H), AX.X)\
                    .then_inc(s2_made, 1)

            dve.memset(neg_half[:], -0.5).then_inc(consts_set, 1)
            dve.memset(ln_scale[:], LN_V_SCALE).then_inc(consts_set, 1)
            dve.memset(exponent[:], -0.5).then_inc(consts_set, 1)
            dve.memset(met_den[:], 1.0).then_inc(consts_set, 1)
            dve.memset(slopes[:, 0:1], 1.0).then_inc(consts_set, 1)
            dve.memset(slopes[:, 1:2], LEAK).then_inc(consts_set, 1)
            dve.memset(hb[:], 1.0).then_inc(consts_set, 1)
            dve.wait_ge(consts_in, 16 * (KD + 4))
            n = 0
            for k in range(KD):
                for i in range(2):
                    prod = att[:, 0, 2 * k + i, :].rearrange("p (h e) -> p h e", h=H)
                    a = sq[:, i, :].rearrange("p (h e) -> p h e", h=H)
                    dve.tensor_tensor(prod, wa[:, k, 0:D].rearrange("p (h e) -> p h e", h=H), a, ALU.mult)\
                        .then_inc(wa_done, 1)
            dve.tensor_copy(sel[:], tail_of(ident[0:TPB * H, 0:TPB * H], P)).then_inc(consts_set, 1)
            dve.wait_ge(wa_done, 2 * KD)
            for k in range(KD):
                for i in range(2):
                    prod = att[:, 0, 2 * k + i, :].rearrange("p (h e) -> p h e", h=H)
                    ins = dve.reduce_sum(wa[:, k, D + i * H:D + (i + 1) * H], prod, AX.X)
            ins.then_inc(consts_set, 1)
            dve.wait_ge(consts_set, 9)
            dve.tensor_tensor(att[:, 0, 0, :], bias_bc[:], bias_bc[:], ALU.mult).then_inc(wa_done, 1)
            dve.wait_ge(wa_done, 2 * KD + 1)
            dve.reduce_sum(worst[:, 4:5], att[:, 0, 0, :], AX.X).then_inc(wa_done, 1)

            add_bias(0, 0)
            with dve.Fori(0, BPB - 1) as p:
                for t in range(1, TPB + 1):
                    add_bias(p * TPB + t, t % TPB, hp_before[t % 2], p if t == TPB else None)
            before_first_g()
            for t in range(1, TPB + 1):
                for jt in range(3 * t - 3, 3 * t):
                    make_g(0, 0, 0, jt)
                add_bias((BPB - 1) * TPB + t, t % TPB, hp_before[t % 2], BPB - 1 if t == TPB else None)
            dve.wait_ge(h_read_dve, JT)
            for jt in range(3 * TPB, JT):
                make_g(0, 0, 0, jt)

            def step(g, more=False, first=False, last=False):
                for h in range(H):
                    u = g * H + h
                    after = (g, h + 1) if h + 1 < H else (g + 1, 0)
                    before = (g, h - 1) if h else (g - 1, H - 1)
                    g_too = not (last and h == H - 1)
                    result = not (first and h == 0)
                    if g_too:
                        before_g(*after, u + 1)
                    for jt in range(JT):
                        if g_too:
                            make_g(*after, u + 1, jt)
                        if jt == 7 and result:
                            reciprocals(u - 1)
                        if jt == 11 and more:
                            add_bias(u + JT + 1, (h + 1) % TPB, p=g + BPB if h == H - 1 else None)
                        if jt == 12 and result:
                            second_terms(*before, u - 1, (h + 1) % 2)
                        if not first and h == 1:
                            if jt == 1:
                                residual(g - 1)
                        if not first and h == 2 and jt == 8:
                            square_sums(g - 1)

            step(0, more=True, first=True)
            with dve.Fori(1, NB - BPB) as g:
                step(g, more=True)
            with dve.Fori(NB - BPB, NB - 1) as g:
                step(g)
            step(NB - 1, last=True)
            u = NB * H - 1
            reciprocals(u)
            second_terms(NB - 1, H - 1, u, u % 2)
            residual(NB - 1)
            square_sums(NB - 1)
            dve.wait_ge(adj_checked, NB * CPB)
            dve.wait_ge(h_read_act, NT + 1)
            dve.wait_ge(wa_done, 2 * KD + 2)
            for i, (met, op) in enumerate(((met_adj, ALU.max), (met_exp, ALU.max), (met_h, ALU.max),
                                           (met_den, ALU.min))):
                dve.tensor_reduce(worst[:, i:i + 1], met[:], AX.X, op).then_inc(viol_step_dve, 1)
            dve.wait_ge(viol_step_dve, 4)
            for i, (most, op) in enumerate(((CH / 4.0, ALU.is_gt), (EXP_SQ, ALU.is_gt), (H_SQ, ALU.is_gt),
                                            (DEN_LEAST * 2.0, ALU.is_lt), (BIAS_SQ, ALU.is_gt))):
                dve.tensor_scalar(broken[:, i:i + 1], worst[:, i:i + 1], most, None, op).then_inc(viol_step_dve, 1)
            dve.wait_ge(viol_step_dve, 9)
            dve.tensor_reduce(broken[:, 5:6], broken[:, 0:5], AX.X, ALU.max).then_inc(met_done, 1)

        @block.tensor
        def _(pe):
            def turn_x(t, slot):
                pe.wait_ge(x_in[slot], (t // 2) * 16 + 16)
                pe.wait_ge(xT_copied, t)
                for k in range(KD):
                    ins = pe.transpose(turn[:, k * P:(k + 1) * P], xin[:, slot, k * P:(k + 1) * P], ident[:])
                ins.then_inc(x_turned, 1)

            def project(t, blocks_split=None, hp=hp, banks=1):
                pe.wait_ge(xT_copied, t + 1)
                pe.wait_ge(exps_made, FIRST + t + 1 - banks)
                if blocks_split is not None:
                    pe.wait_ge(na_split, FIRST + blocks_split)
                for k in range(KD):
                    ins = pe.matmul(hp[:, 0:D + 2 * H], xT[:, k, :], wa[:, k, :], start=(k == 0), stop=(k == KD - 1))
                ins.then_inc(h_made, 1)

            def turn_na(p):
                pe.wait_ge(h_read_dve, p * TPB + TPB)
                pe.wait_ge(exps_made, FIRST + p * TPB + TPB)
                pe.transpose(na_turn, na_c[:].rearrange("p h t -> p (h t)"), ident[:]).then_inc(na_turned, 1)

            def spread_na(g, h, u):
                if not (isinstance(u, int) and u < 2):
                    pe.wait_ge(g_made, (u - 1) * JT)
                if h == 0:
                    pe.wait_ge(na_split, FIRST + g + 1)
                stand(pe)
                for it in range(TPB):
                    for s in range(2):
                        rhs = na_t[:, bass.ds(g % NA_SLOTS, 1), s, :].rearrange("p a i -> p (a i)")
                        ins = pe.matmul(na[:, h % 2, it * P:(it + 1) * P], sel[:, h * TPB + it, :], rhs,
                                        start=(s == 0), stop=(s == 1))
                ins.then_inc(na_made, 1)

            def sums(batch_half, g_half, h, u, it):
                s = h % 2
                out = region(s, it)
                for jt in range(JT):
                    if it == 0 and jt % 4 == 0:
                        pe.wait_ge(g_made, u * JT + jt + 4)
                    v = vh[:, batch_half * JT + jt, h, :, :, :]
                    gg = g_sb[:, s, jt, it * P:(it + 1) * P]
                    mm = mt[:, g_half, jt, it * P:(it + 1) * P]
                    for part in range(2):
                        pe.matmul(out[:, 0:2 * E1], gg, v[:, part, :, :].rearrange("p f e -> p (f e)"),
                                  start=(jt == 0 and part == 0), stop=False, skip_group_check=True)
                    for part in range(2):
                        ins = pe.matmul(out[:, 2 * E1:RW], mm, v[:, part, 1, :], start=False,
                                        stop=(jt == JT - 1 and part == 1), skip_group_check=True)
                return ins

            pe.wait_ge(consts_set, 9)
            turn_x(0, 0)
            project(0)
            turn_x(1, 1)
            def prep(p):
                for t in range(1, TPB + 1):
                    T = p * TPB + t
                    if t == TPB:
                        turn_na(p)
                    project(T, p if t == 2 else None, hp_before[t % 2], 2)
                    turn_x(T + 1, (t + 1) % 2)

            with pe.Fori(0, BPB - 1) as p:
                prep(p)
            spread_na(0, 0, 0)
            spread_na(0, 1, 1)
            prep(BPB - 1)

            def step(g, batch_half, more=False, last=False):
                for k in range(2 * H):
                    h, g_half = k % H, k // H
                    u = g * H + k
                    if more:
                        T = u + JT + 1
                    if k == 0:
                        pe.wait_ge(vh_done, (g // BPB + 1) * JT)
                    for it in range(TPB):
                        ins = sums(batch_half, g_half, h, u, it)
                        if it == 0 and not (last and k >= 2 * H - 2):
                            spread_na(g + (k + 2) // H, (k + 2) % H, u + 2)
                        if it == 0 and more and h == H - 1:
                            turn_na(g + g_half + BPB)
                        if it == 0 and more:
                            project(T, g + g_half + BPB if h == 0 else None)
                        if it == 1 and more:
                            turn_x(T + 1, h % 2)
                    ins.then_inc(unit_done, 1)
                    pe.wait_ge(att_made, FIRST + u)

            if B > 2:
                with pe.Fori(0, B // 2 - 1) as pair:
                    for half in range(2):
                        with pe.Fori(0, BPB // 2) as q:
                            step(pair * (2 * BPB) + q * 2 + half * BPB, half, more=True)
            with pe.Fori(0, BPB // 2) as q:
                step(q * 2 + NB - 2 * BPB, 0, more=True)
            with pe.Fori(0, BPB // 2 - 1) as q:
                step(q * 2 + NB - BPB, 1)
            step(NB - 2, 1, last=True)


def general_path(nc, io, viol_i, sems):
    x, adj, W = io["x"], io["adj"], io["W"]
    B, N, D, H, E = dims(x, adj, W)
    T = io["a_src"].shape[1]
    JT = N // P
    NT = B * JT
    KD = D // P
    HT = H * T
    PC = D + HT
    CW = min(512, N)
    CK = N // CW
    NEG = -1e9

    x_t = x.rearrange("b (t p) d -> p (b t) d", p=P)
    out_t = io["out"].rearrange("b (t p) d -> p (b t) d", p=P)
    adj_t = adj.rearrange("b (t p) n -> p (b t) n", p=P)
    heads_t = io["hu"][:, 0:D].rearrange("(t p) c -> p t c", p=P)

    with ExitStack() as ctx:
        def sb(name, shape, dt=F32):
            return ctx.enter_context(nc.sbuf_tensor(name, shape, dt))

        def psum(name, shape, dt=F32):
            return ctx.enter_context(nc.psum_tensor(name, shape, dt))

        def sem(name):
            return sems.enter_context(nc.semaphore(name))

        ident = sb("g_ident", [P, P])
        wp = sb("g_wp", [P, KD, PC])
        wd = sb("g_wd", [P, KD, HT])
        wd_rep = sb("g_wd_rep", [P, KD, T, P])
        a_bc = sb("g_a_bc", [P, 2, HT, E])
        prod = sb("g_prod", [P, HT, E])
        bias_bc = sb("g_bias", [P, D])
        gamma_bc = sb("g_gamma", [P, D])
        beta_bc = sb("g_beta", [P, D])
        half_neg = sb("g_half_neg", [P, 1])
        xin = sb("g_xin", [P, D])
        xT = sb("g_xT", [P, KD, N])
        xT_tile = sb("g_xT_tile", [P, KD, P])
        hs = sb("g_h", [P, JT, PC])
        b_bc = sb("g_b_bc", [P, T, N])
        adj_i = sb("g_adj_i", [P, N], I32)
        adj_f = sb("g_adj_f", [P, N])
        mask = sb("g_mask", [P, N])
        w = sb("g_w", [P, N])
        term = sb("g_term", [P, N])
        pr = sb("g_p", [P, N])
        prT = sb("g_pT", [P, JT, P])
        st = sb("g_st", [P, 12])
        o = sb("g_o", [P, E])
        c = sb("g_c", [P, E])
        z = sb("g_z", [P, D])
        zc = sb("g_zc", [P, D])
        xr = sb("g_xr", [P, D])

        ps_x = psum("g_ps_x", [P, 512])
        ps_h = psum("g_ps_h", [P, 512])
        ps_b = psum("g_ps_b", [P, 512])
        ps_p = psum("g_ps_p", [P, 512])
        ps_o = psum("g_ps_o", [P, 512])

        consts_in = sem("g_consts_in")
        consts_set = sem("g_consts_set")
        x_in = sem("g_x_in")
        x_turned = sem("g_x_turned")
        xT_copied = sem("g_xT_copied")
        h_made = sem("g_h_made")
        h_copied = sem("g_h_copied")
        rep_made = sem("g_rep_made")
        b_made = sem("g_b_made")
        b_copied = sem("g_b_copied")
        adj_in = sem("g_adj_in")
        adj_read = sem("g_adj_read")
        dve_step = sem("g_dve_step")
        w_made = sem("g_w_made")
        p_made = sem("g_p_made")
        p_turned = sem("g_p_turned")
        pT_copied = sem("g_pT_copied")
        sum_made = sem("g_sum_made")
        var_made = sem("g_var_made")
        std_made = sem("g_std_made")
        head_made = sem("g_head_made")
        head_stored = sem("g_head_stored")
        z_in = sem("g_z_in")
        row_var = sem("g_row_var")
        row_std = sem("g_row_std")
        row_scaled = sem("g_row_scaled")
        row_made = sem("g_row_made")
        row_stored = sem("g_row_stored")
        stood = {e.engine: sem(f"g_stood_{n}") for n, e in
                 (("sp", nc.sync), ("pool", nc.gpsimd), ("act", nc.scalar), ("dve", nc.vector), ("pe", nc.tensor))}

        def stand(eng):
            eng.sem_inc(stood[eng.engine], 1)

        from_first = (x_turned, adj_read, row_made, xT_copied, h_copied, b_copied, pT_copied, head_made,
                      b_made, w_made, p_turned, sum_made, p_made, head_stored, row_stored)

        block = ctx.enter_context(nc.Block())
        TILE_STEPS = 3 * T + 13

        @block.sync
        def _(sp):
            with sp.If(sp.value_load(viol_i[0:1, 0:1], min_val=0, max_val=1) > 0):
                for first in from_first:
                    sp.sem_inc(first, FIRST)
                sp.dma_start(ident[:], io["eye"]).then_inc(consts_in, 16)
                for k in range(KD):
                    dst = wp[:, k, 0:D].rearrange("p (h e) -> p h e", h=H)
                    sp.dma_start(dst, W.rearrange("h (k p) e -> k p h e", p=P)[k]).then_inc(consts_in, 16)
                for tile, src in ((bias_bc, io["bias"]), (gamma_bc, io["gamma"]), (beta_bc, io["beta"])):
                    dst = tile[:].rearrange("p (h e) -> p h e", h=H)
                    sp.dma_start(dst, src.partition_broadcast(P)).then_inc(consts_in, 16)
                for i, src in enumerate((io["a_src"], io["a_dst"])):
                    sp.dma_start(a_bc[:, i, :, :], src.rearrange("h t e -> (h t) e").partition_broadcast(P))\
                        .then_inc(consts_in, 16)
                with sp.Fori(0, B) as b:
                    with sp.Fori(0, JT) as t:
                        sp.wait_ge(x_turned, FIRST + b * JT + t)
                        stand(sp)
                        sp.dma_start(xin[:].unsqueeze(1), x_t[:, bass.ds(b * JT + t, 1), :]).then_inc(x_in, 16)
                    with sp.Fori(0, H) as h:
                        with sp.Fori(0, JT) as t:
                            n = (b * H + h) * JT + t
                            sp.wait_ge(adj_read, FIRST + n)
                            stand(sp)
                            sp.dma_start(adj_i[:].unsqueeze(1), adj_t[:, bass.ds(b * JT + t, 1), :])\
                                .then_inc(adj_in, 16)
                            sp.wait_ge(head_made, FIRST + n + 1)
                            stand(sp)
                            dst = heads_t[:, bass.ds(b * JT + t, 1), bass.ds(h * E, E)]
                            sp.dma_start(dst, o[:].unsqueeze(1)).then_inc(head_stored, 16)
                sp.wait_ge(head_stored, FIRST + B * H * JT * 16)
                with sp.Fori(0, NT) as t:
                    sp.wait_ge(row_made, FIRST + t)
                    stand(sp)
                    sp.dma_start(z[:].unsqueeze(1), heads_t[:, bass.ds(t, 1), :]).then_inc(z_in, 16)
                    sp.dma_start(xr[:].unsqueeze(1), x_t[:, bass.ds(t, 1), :]).then_inc(z_in, 16)
                    sp.wait_ge(row_made, FIRST + t + 1)
                    stand(sp)
                    sp.dma_start(out_t[:, bass.ds(t, 1), :], zc[:].unsqueeze(1)).then_inc(row_stored, 16)
                sp.wait_ge(row_stored, FIRST + NT * 16)

        @block.tensor
        def _(pe):
            with pe.If(pe.value_load(viol_i[0:1, 0:1], min_val=0, max_val=1) > 0):
                pe.wait_ge(consts_set, 2)
                pe.wait_ge(consts_in, 16 * (KD + 6))
                with pe.Fori(0, B) as b:
                    with pe.Fori(0, JT) as t:
                        n = b * JT + t
                        pe.wait_ge(x_in, n * 16 + 16)
                        pe.wait_ge(xT_copied, FIRST + n * 2)
                        stand(pe)
                        for k in range(KD):
                            ins = pe.transpose(ps_x[:, k * P:(k + 1) * P], xin[:, k * P:(k + 1) * P], ident[:])
                        ins.then_inc(x_turned, 1)
                        pe.wait_ge(xT_copied, FIRST + n * 2 + 2)
                        pe.wait_ge(h_copied, FIRST + n)
                        stand(pe)
                        for k in range(KD):
                            ins = pe.matmul(ps_h[:, 0:PC], xT_tile[:, k, :], wp[:, k, :],
                                            start=(k == 0), stop=(k == KD - 1))
                        ins.then_inc(h_made, 1)
                    with pe.Fori(0, H) as h:
                        pe.wait_ge(rep_made, b * H + h + 1)
                        pe.wait_ge(xT_copied, FIRST + (b * JT + JT) * 2)
                        stand(pe)
                        for q in range(T * CK):
                            ty, ch = q // CK, q % CK
                            pe.wait_ge(b_copied, FIRST + (b * H + h) * (T * CK) + q)
                            stand(pe)
                            for k in range(KD):
                                ins = pe.matmul(ps_b[:, 0:CW], wd_rep[:, k, ty, :], xT[:, k, ch * CW:(ch + 1) * CW],
                                                start=(k == 0), stop=(k == KD - 1))
                            ins.then_inc(b_made, 1)
                        with pe.Fori(0, JT) as t:
                            n = (b * H + h) * JT + t
                            pe.wait_ge(p_made, FIRST + n + 1)
                            pe.wait_ge(h_copied, FIRST + b * JT + JT)
                            stand(pe)
                            for ch in range(CK):
                                pe.wait_ge(pT_copied, FIRST + n * CK + ch)
                                stand(pe)
                                for q in range(CW // P):
                                    j = ch * (CW // P) + q
                                    ins = pe.transpose(ps_p[:, q * P:(q + 1) * P], pr[:, j * P:(j + 1) * P], ident[:])
                                ins.then_inc(p_turned, 1)
                            pe.wait_ge(pT_copied, FIRST + n * CK + CK)
                            pe.wait_ge(head_made, FIRST + n)
                            stand(pe)
                            for j in range(JT):
                                ins = pe.matmul(ps_o[:, 0:E], prT[:, j, :], hs[:, j, bass.ds(h * E, E)],
                                                start=(j == 0), stop=(j == JT - 1))
                            ins.then_inc(sum_made, 1)

        @block.scalar
        def _(act):
            with act.If(act.value_load(viol_i[0:1, 0:1], min_val=0, max_val=1) > 0):
                with act.Fori(0, B) as b:
                    with act.Fori(0, JT) as t:
                        n = b * JT + t
                        act.wait_ge(x_turned, FIRST + n + 1)
                        act.wait_ge(b_made, FIRST + b * H * T * CK)
                        stand(act)
                        turned = ps_x[:, 0:D].rearrange("p (k i) -> p k i", k=KD)
                        act.activation(xT[:, :, bass.ds(t * P, P)], turned, ACT.Copy).then_inc(xT_copied, 1)
                        act.activation(xT_tile[:], turned, ACT.Copy).then_inc(xT_copied, 1)
                        act.wait_ge(h_made, n + 1)
                        act.wait_ge(head_made, FIRST + b * H * JT)
                        stand(act)
                        act.activation(hs[:, bass.ds(t, 1), :].rearrange("p a c -> p (a c)"), ps_h[:, 0:PC], ACT.Copy)\
                            .then_inc(h_copied, 1)
                    with act.Fori(0, H) as h:
                        act.wait_ge(w_made, FIRST + (b * H + h) * JT)
                        stand(act)
                        for q in range(T * CK):
                            ty, ch = q // CK, q % CK
                            act.wait_ge(b_made, FIRST + (b * H + h) * (T * CK) + q + 1)
                            stand(act)
                            act.activation(b_bc[:, ty, ch * CW:(ch + 1) * CW], ps_b[:, 0:CW], ACT.Copy)\
                                .then_inc(b_copied, 1)
                        with act.Fori(0, JT) as t:
                            n = (b * H + h) * JT + t
                            act.wait_ge(w_made, FIRST + n + 1)
                            act.wait_ge(p_turned, FIRST + n * CK)
                            act.wait_ge(head_made, FIRST + n)
                            stand(act)
                            act.activation(pr[:], w[:], ACT.Exp, bias=st[:, 0:1], accum_out=st[:, 1:2]).then_inc(p_made, 1)
                            for ch in range(CK):
                                act.wait_ge(p_turned, FIRST + n * CK + ch + 1)
                                act.wait_ge(sum_made, FIRST + n)
                                stand(act)
                                dst = prT[:, ch * (CW // P):(ch + 1) * (CW // P), :]
                                act.activation(dst, ps_p[:, 0:CW].rearrange("p (q i) -> p q i", i=P), ACT.Copy)\
                                    .then_inc(pT_copied, 1)

        @block.vector
        def _(dve):
            with dve.If(dve.value_load(viol_i[0:1, 0:1], min_val=0, max_val=1) > 0):
                dve.memset(half_neg[:], -0.5).then_inc(consts_set, 1)
                dve.wait_ge(consts_in, 16 * (KD + 6))
                n = 0
                for i, dst in enumerate((wp, wd)):
                    for k in range(KD):
                        for h in range(H):
                            wk = wp[:, k, h * E:(h + 1) * E].unsqueeze(1).to_broadcast([P, T, E])
                            if n:
                                dve.wait_ge(dve_step, n)
                            dve.tensor_tensor(prod[:, 0:T, :], wk, a_bc[:, i, h * T:(h + 1) * T, :], ALU.mult)\
                                .then_inc(dve_step, 1)
                            dve.wait_ge(dve_step, n + 1)
                            off = (D if i == 0 else 0) + h * T
                            dve.reduce_sum(dst[:, k, off:off + T], prod[:, 0:T, :], AX.X).then_inc(dve_step, 1)
                            n += 2
                dve.wait_ge(dve_step, n)
                dve.memset(c[:], 0.0).then_inc(consts_set, 1)
                first = n
                with dve.Fori(0, B) as b:
                    with dve.Fori(0, H) as h:
                        dve.wait_ge(b_made, FIRST + (b * H + h) * (T * CK))
                        stand(dve)
                        src = wd[:, :, bass.ds(h * T, T)]
                        for k in range(KD):
                            ins = dve.tensor_copy(wd_rep[:, k, :, :], src[:, k, :].unsqueeze(2).to_broadcast([P, T, P]))
                        ins.then_inc(rep_made, 1)
                        dve.wait_ge(b_copied, FIRST + (b * H + h + 1) * (T * CK))
                        dve.wait_ge(h_copied, FIRST + b * JT + JT)
                        stand(dve)
                        with dve.Fori(0, JT) as t:
                            m = (b * H + h) * JT + t
                            s0 = m * TILE_STEPS + first

                            def done(i):
                                dve.wait_ge(dve_step, s0 + i)
                                stand(dve)

                            dve.wait_ge(adj_in, m * 16 + 16)
                            dve.wait_ge(p_made, FIRST + m)
                            stand(dve)
                            dve.tensor_copy(adj_f[:], adj_i[:]).then_inc(adj_read, 1)
                            dve.wait_ge(adj_read, FIRST + m + 1)
                            stand(dve)
                            dve.tensor_scalar(w[:], adj_f[:], 0.0, 0.0, ALU.mult, ALU.mult).then_inc(dve_step, 1)
                            for ty in range(T):
                                done(3 * ty + 1)
                                dve.tensor_scalar(mask[:], adj_f[:], float(ty + 1), None, ALU.is_equal)\
                                    .then_inc(dve_step, 1)
                                done(3 * ty + 2)
                                a = hs[:, bass.ds(t, 1), bass.ds(h * T + (D + ty), 1)].rearrange("p a c -> p (a c)")
                                dve.scalar_tensor_tensor(out=term[:], in0=b_bc[:, ty, :], scalar=a, in1=mask[:],
                                                         op0=ALU.add, op1=ALU.mult).then_inc(dve_step, 1)
                                done(3 * ty + 3)
                                dve.tensor_tensor(w[:], w[:], term[:], ALU.add).then_inc(dve_step, 1)
                            done(3 * T + 1)
                            dve.scalar_tensor_tensor(out=term[:], in0=w[:], scalar=LEAK, in1=w[:],
                                                     op0=ALU.mult, op1=ALU.max).then_inc(dve_step, 1)
                            dve.tensor_scalar(mask[:], adj_f[:], 0.0, NEG, ALU.is_equal, ALU.mult).then_inc(dve_step, 1)
                            done(3 * T + 3)
                            dve.tensor_tensor(w[:], term[:], mask[:], ALU.add).then_inc(dve_step, 1)
                            done(3 * T + 4)
                            dve.tensor_reduce(st[:, 2:3], w[:], AX.X, ALU.max).then_inc(dve_step, 1)
                            done(3 * T + 5)
                            dve.tensor_scalar(st[:, 0:1], st[:, 2:3], -1.0, None, ALU.mult).then_inc(w_made, 1)
                            dve.wait_ge(p_made, FIRST + m + 1)
                            dve.wait_ge(sum_made, FIRST + m + 1)
                            dve.wait_ge(head_stored, FIRST + m * 16)
                            stand(dve)
                            dve.reciprocal(st[:, 3:4], st[:, 1:2]).then_inc(dve_step, 1)
                            done(3 * T + 6)
                            hb = bass.ds(h * E, E)
                            dve.scalar_tensor_tensor(out=o[:], in0=ps_o[:, 0:E], scalar=st[:, 3:4],
                                                     in1=bias_bc[:, hb], op0=ALU.mult, op1=ALU.add).then_inc(dve_step, 1)
                            done(3 * T + 7)
                            hh = hs[:, bass.ds(t, 1), hb].rearrange("p a e -> p (a e)")
                            dve.scalar_tensor_tensor(out=c[:], in0=o[:], scalar=0.0, in1=hh,
                                                     op0=ALU.max, op1=ALU.add).then_inc(dve_step, 1)
                            done(3 * T + 8)
                            dve.reduce_sum(st[:, 4:5], c[:], AX.X).then_inc(dve_step, 1)
                            done(3 * T + 9)
                            dve.tensor_scalar(st[:, 5:6], st[:, 4:5], -1.0 / E, None, ALU.mult).then_inc(dve_step, 1)
                            done(3 * T + 10)
                            dve.tensor_scalar(c[:], c[:], st[:, 5:6], None, ALU.add).then_inc(dve_step, 1)
                            done(3 * T + 11)
                            dve.tensor_tensor(o[:], c[:], c[:], ALU.mult).then_inc(dve_step, 1)
                            done(3 * T + 12)
                            dve.reduce_sum(st[:, 6:7], o[:], AX.X).then_inc(dve_step, 1)
                            done(3 * T + 13)
                            dve.tensor_scalar(st[:, 7:8], st[:, 6:7], 1.0 / E, EPS_HEAD, ALU.mult, ALU.add)\
                                .then_inc(var_made, 1)
                            dve.wait_ge(std_made, m + 1)
                            stand(dve)
                            dve.scalar_tensor_tensor(out=o[:], in0=c[:], scalar=st[:, 8:9], in1=gamma_bc[:, hb],
                                                     op0=ALU.mult, op1=ALU.mult).then_inc(var_made, 1)
                            dve.wait_ge(var_made, m * 2 + 2)
                            stand(dve)
                            dve.tensor_tensor(o[:], o[:], beta_bc[:, hb], ALU.add).then_inc(head_made, 1)
                with dve.Fori(0, NT) as t:
                    def done_row(i):
                        dve.wait_ge(row_var, t * 6 + i)
                        stand(dve)

                    dve.wait_ge(z_in, t * 32 + 32)
                    stand(dve)
                    dve.tensor_tensor(z[:], z[:], xr[:], ALU.add).then_inc(row_var, 1)
                    done_row(1)
                    dve.reduce_sum(st[:, 9:10], z[:], AX.X).then_inc(row_var, 1)
                    done_row(2)
                    dve.tensor_scalar(st[:, 10:11], st[:, 9:10], -1.0 / D, None, ALU.mult).then_inc(row_var, 1)
                    dve.wait_ge(row_stored, FIRST + t * 16)
                    done_row(3)
                    dve.tensor_scalar(z[:], z[:], st[:, 10:11], None, ALU.add).then_inc(row_var, 1)
                    done_row(4)
                    dve.tensor_tensor(zc[:], z[:], z[:], ALU.mult).then_inc(row_var, 1)
                    done_row(5)
                    dve.reduce_sum(st[:, 9:10], zc[:], AX.X).then_inc(row_var, 1)
                    dve.wait_ge(row_std, t + 1)
                    stand(dve)
                    dve.tensor_scalar(zc[:], z[:], st[:, 11:12], None, ALU.mult).then_inc(row_made, 1)

        @block.gpsimd
        def _(pool):
            with pool.If(pool.value_load(viol_i[0:1, 0:1], min_val=0, max_val=1) > 0):
                pool.wait_ge(consts_set, 1)
                with pool.Fori(0, B * H * JT) as m:
                    pool.wait_ge(var_made, m * 2 + 1)
                    stand(pool)
                    pool.tensor_tensor(st[:, 8:9], st[:, 7:8], half_neg[:], ALU.pow).then_inc(std_made, 1)
                with pool.Fori(0, NT) as t:
                    pool.wait_ge(row_var, t * 6 + 6)
                    stand(pool)
                    pool.tensor_scalar(st[:, 7:8], st[:, 9:10], 1.0 / D, EPS_ROW, ALU.mult, ALU.add)\
                        .then_inc(row_scaled, 1)
                    pool.wait_ge(row_scaled, t + 1)
                    stand(pool)
                    pool.tensor_tensor(st[:, 11:12], st[:, 7:8], half_neg[:], ALU.pow).then_inc(row_std, 1)




_SHORT = {"x": "x", "adj": "adj", "L0_gnn_W": "W", "L0_gnn_a_src": "a_src", "L0_gnn_a_dst": "a_dst",
          "L0_gnn_bias": "bias", "L0_gnn_ln_gamma": "gamma", "L0_gnn_ln_beta": "beta"}


def gat_layer(nc, io):
    with nc.sbuf_tensor("viol_i", [P, 1], I32) as viol_i, ExitStack() as sems:
        main_path(nc, io, viol_i, sems)
        general_path(nc, io, viol_i, sems)


def kernel(**inputs):
    import numpy as np
    import concourse.bacc as bacc
    from concourse.bass_utils import run_bass_kernel_spmd

    nc = bacc.Bacc("TRN2", target_bir_lowering=False, num_devices=1)
    arrays, io = {}, {}
    for name, short in _SHORT.items():
        a = np.ascontiguousarray(inputs[name])
        arrays[f"in_{short}"] = a
        io[short] = nc.dram_tensor(f"in_{short}", a.shape, mybir.dt.from_np(a.dtype), kind="ExternalInput").ap()
    arrays["in_eye"] = np.eye(P, dtype=np.float32)
    io["eye"] = nc.dram_tensor("in_eye", (P, P), F32, kind="ExternalInput").ap()
    B, N, D, H, E = dims(io["x"], io["adj"], io["W"])
    io["hu"] = nc.dram_tensor("scratch_hu", (B * N, D + 4 * H), F32, kind="Internal").ap()
    io["out"] = nc.dram_tensor("out", (B, N, D), F32, kind="ExternalOutput").ap()
    gat_layer(nc, io)
    r = run_bass_kernel_spmd(nc, [arrays], core_ids=[0])
    return r.results[0]["out"]
```
